# Optimizing a Trainium2 kernel written in Bass

```python
import numpy as np
import jax
import jax.numpy as jnp

def _softmax(x, axis=-1):
    return jax.nn.softmax(x, axis=axis)

def _gelu(x):
    return jax.nn.gelu(x, approximate=True)

def _silu(x):
    return jax.nn.silu(x)

def _sigmoid(x):
    return jax.nn.sigmoid(x)

def _layernorm(x, axis=-1, eps=1e-05):
    m = jnp.mean(x, axis=axis, keepdims=True)
    v = jnp.var(x, axis=axis, keepdims=True)
    return (x - m) / jnp.sqrt(v + eps)

def _scatter_add(tgt, idx, src, axis=0):
    return tgt.at[idx].add(src)

def _segment_sum(src, seg, n):
    return jax.ops.segment_sum(src, seg, n)
kernel_name = 'mk_audio_tower_d2_tok_audfeat512_r4_78572e'

def setup_inputs(seed: int=0):
    np.random.seed(seed)
    _w = jnp.asarray

    def _rec_inputs():
        import jax
        import jax.numpy as jnp
        _rk = jax.random.key(seed)
        x = -0.000392918 + 0.999932 * jax.random.normal(jax.random.fold_in(_rk, 1), (8, 750, 128), jnp.float32)
        return x
    x = _rec_inputs()

    def _L0_tok_setup():
        import jax, jax.numpy as jnp
        import numpy as np
        from jax import lax
        B, T, D = (32, 256, 128)
        UNITS, WINDOW = (128, 3)
        key = jax.random.key(seed)
        k1, k2 = jax.random.split(key)
        x = jax.random.normal(k1, (B, T, D), dtype=jnp.float32)
        kernel = jax.random.normal(k2, (WINDOW, D, UNITS * 3), dtype=jnp.float32) * 0.05
        return {'x': x, 'kernel': kernel}
    _L0_tok_all = _L0_tok_setup()
    _L0_tok_in = {k: v for k, v in _L0_tok_all.items() if k in ('kernel',)}
    del _L0_tok_all

    def _L0_attn_setup():
        import jax, jax.numpy as jnp
        import numpy as np
        key = jax.random.key(seed)
        x = jax.random.normal(key, (8, 512, 128), dtype=jnp.float32)
        return {'x': x}
    _L0_attn_all = _L0_attn_setup()
    _L0_attn_in = {k: v for k, v in _L0_attn_all.items() if k in ()}
    del _L0_attn_all

    def _L0_ffn_setup():
        import jax, jax.numpy as jnp
        import numpy as np
        MARK_AX, OP_ADD, OP_SUB = (0, 1, 2)
        ALU_LO, ALU_HI = (16, 32)
        AX_CARRY_LO, AX_CARRY_HI = (48, 64)
        OPCODE_BASE = 80
        OUTPUT_LO, OUTPUT_HI, CARRY = (128, 144, 160)
        NIB_A, NIB_B, OP_START = (0, 1, 10)
        RESULT, CARRY_OUT = (100, 101)
        GE_POS, GE_DIM = (8, 160)
        OPC_ADD, OPC_SUB = (25, 26)
        B, S, D = (8, 1024, 128)

        def _decode_nibble(x, base):
            return jnp.argmax(x[..., base:base + 16] > 0.5, axis=-1).astype(x.dtype)

        def _pipeline(h, W, b):
            for i in range(3):
                h = jnp.einsum('bspd,od->bspo', h, W[i]) + b[i]
                if i < 2:
                    h = jax.nn.relu(h)
            return h
        key = jax.random.key(seed)
        kx, k1, k2, k3, k4 = jax.random.split(key, 5)
        x_bd = jax.random.uniform(kx, (B, S, D), dtype=jnp.float32)
        Wa = jax.random.normal(k1, (3, GE_DIM, GE_DIM), dtype=jnp.float32) * 0.05
        ba = jax.random.normal(k2, (3, GE_DIM), dtype=jnp.float32) * 0.05
        Ws = jax.random.normal(k3, (3, GE_DIM, GE_DIM), dtype=jnp.float32) * 0.05
        bs = jax.random.normal(k4, (3, GE_DIM), dtype=jnp.float32) * 0.05
        return {'x_bd': x_bd, 'Wa': Wa, 'ba': ba, 'Ws': Ws, 'bs': bs}
    _L0_ffn_all = _L0_ffn_setup()
    _L0_ffn_in = {k: v for k, v in _L0_ffn_all.items() if k in ('Wa', 'ba', 'Ws', 'bs')}
    del _L0_ffn_all

    def _L1_attn_setup():
        import jax, jax.numpy as jnp
        import numpy as np
        EMB_DIM = 128
        N_HEAD = 8
        HEAD_DIM = EMB_DIM // N_HEAD
        SEQ_LEN = 512
        BATCH = 4
        key = jax.random.key(seed)
        k1, k2, k3 = jax.random.split(key, 3)
        emb = jax.random.normal(k1, (SEQ_LEN, BATCH, EMB_DIM), dtype=jnp.float32)
        W = jax.random.normal(k2, (3 * EMB_DIM, EMB_DIM), dtype=jnp.float32) * 0.02
        b = jax.random.normal(k3, (3 * EMB_DIM,), dtype=jnp.float32) * 0.02
        return {'emb': emb, 'W': W, 'b': b}
    _L1_attn_all = _L1_attn_setup()
    _L1_attn_in = {k: v for k, v in _L1_attn_all.items() if k in ('W', 'b')}
    del _L1_attn_all

    def _L1_ffn_setup():
        import jax, jax.numpy as jnp
        import numpy as np
        B, S, D = (8, 512, 128)
        FF = 512
        E = 8
        key = jax.random.key(seed)
        ks = jax.random.split(key, 7)
        s = 1.0 / np.sqrt(D)
        sf = 1.0 / np.sqrt(FF)
        return {'x': jax.random.normal(ks[0], (B, S, D), dtype=jnp.float32), 'Wg': jax.random.uniform(ks[1], (D, E), jnp.float32, -s, s), 'bg': jax.random.uniform(ks[2], (E,), jnp.float32, -s, s), 'W1': jax.random.uniform(ks[3], (E, D, FF), jnp.float32, -s, s), 'b1': jax.random.uniform(ks[4], (E, FF), jnp.float32, -s, s), 'W2': jax.random.uniform(ks[5], (E, FF, D), jnp.float32, -sf, sf), 'b2': jax.random.uniform(ks[6], (E, D), jnp.float32, -sf, sf)}
    _L1_ffn_all = _L1_ffn_setup()
    _L1_ffn_in = {k: v for k, v in _L1_ffn_all.items() if k in ('Wg', 'bg', 'W1', 'b1', 'W2', 'b2')}
    del _L1_ffn_all
    return {'x': x, 'L0_tok_kernel': _L0_tok_in['kernel'], 'L0_ffn_Wa': _L0_ffn_in['Wa'], 'L0_ffn_ba': _L0_ffn_in['ba'], 'L0_ffn_Ws': _L0_ffn_in['Ws'], 'L0_ffn_bs': _L0_ffn_in['bs'], 'L1_attn_W': _L1_attn_in['W'], 'L1_attn_b': _L1_attn_in['b'], 'L1_ffn_Wg': _L1_ffn_in['Wg'], 'L1_ffn_bg': _L1_ffn_in['bg'], 'L1_ffn_W1': _L1_ffn_in['W1'], 'L1_ffn_b1': _L1_ffn_in['b1'], 'L1_ffn_W2': _L1_ffn_in['W2'], 'L1_ffn_b2': _L1_ffn_in['b2']}

def reference(x, L0_tok_kernel, L0_ffn_Wa, L0_ffn_ba, L0_ffn_Ws, L0_ffn_bs, L1_attn_W, L1_attn_b, L1_ffn_Wg, L1_ffn_bg, L1_ffn_W1, L1_ffn_b1, L1_ffn_W2, L1_ffn_b2):
    import jax
    import jax.numpy as jnp

    def _L0_tok_ref(x, kernel):
        import jax, jax.numpy as jnp
        import numpy as np
        from jax import lax
        B, T, D = (32, 256, 128)
        UNITS, WINDOW = (128, 3)
        units = kernel.shape[2] // 3
        conv = lax.conv_general_dilated(x, kernel, window_strides=(1,), padding='VALID', dimension_numbers=('NWC', 'WIO', 'NWC'))
        Z = conv[..., :units]
        F = conv[..., units:2 * units]
        O = conv[..., 2 * units:]
        z = jnp.tanh(Z)
        f = jax.nn.sigmoid(F)
        o = jax.nn.sigmoid(O)

        def step(c, zfo):
            z_t, f_t, o_t = zfo
            c_t = f_t * c + (1.0 - f_t) * z_t
            return (c_t, o_t * c_t)
        c0 = jnp.zeros((x.shape[0], units), dtype=x.dtype)
        zf = (z.transpose(1, 0, 2), f.transpose(1, 0, 2), o.transpose(1, 0, 2))
        _, hs = lax.scan(step, c0, zf)
        return hs.transpose(1, 0, 2)

    def _L0_attn_ref(x):
        import jax, jax.numpy as jnp
        import numpy as np
        m = jnp.einsum('bnd,bmd->bnm', x, x)
        n = jax.nn.softmax(m, axis=-1)
        o = jnp.einsum('bnm,bmd->bnd', n, x)
        return o * x

    def _L0_ffn_ref(x_bd, Wa, ba, Ws, bs):
        import jax, jax.numpy as jnp
        import numpy as np
        MARK_AX, OP_ADD, OP_SUB = (0, 1, 2)
        ALU_LO, ALU_HI = (16, 32)
        AX_CARRY_LO, AX_CARRY_HI = (48, 64)
        OPCODE_BASE = 80
        OUTPUT_LO, OUTPUT_HI, CARRY = (128, 144, 160)
        NIB_A, NIB_B, OP_START = (0, 1, 10)
        RESULT, CARRY_OUT = (100, 101)
        GE_POS, GE_DIM = (8, 160)
        OPC_ADD, OPC_SUB = (25, 26)
        B, S, D = (8, 1024, 128)

        def _decode_nibble(x, base):
            return jnp.argmax(x[..., base:base + 16] > 0.5, axis=-1).astype(x.dtype)

        def _pipeline(h, W, b):
            for i in range(3):
                h = jnp.einsum('bspd,od->bspo', h, W[i]) + b[i]
                if i < 2:
                    h = jax.nn.relu(h)
            return h
        x = x_bd
        Bsz, seq, _ = x.shape
        x_ge = jnp.zeros((Bsz, seq, GE_POS, GE_DIM), dtype=x.dtype)
        x_ge = x_ge.at[..., 0, NIB_A].set(_decode_nibble(x, ALU_LO))
        x_ge = x_ge.at[..., 1, NIB_A].set(_decode_nibble(x, ALU_HI))
        x_ge = x_ge.at[..., 0, NIB_B].set(_decode_nibble(x, AX_CARRY_LO))
        x_ge = x_ge.at[..., 1, NIB_B].set(_decode_nibble(x, AX_CARRY_HI))
        x_ge = x_ge.at[..., :, OP_START + OPC_ADD].set(x[..., OPCODE_BASE + OPC_ADD][..., None])
        x_ge = x_ge.at[..., :, OP_START + OPC_SUB].set(x[..., OPCODE_BASE + OPC_SUB][..., None])
        mark = x[..., MARK_AX] > 0.5
        m_add = mark & (x[..., OP_ADD] > 0.5)
        m_sub = mark & ~(x[..., OP_ADD] > 0.5) & (x[..., OP_SUB] > 0.5)
        active = (m_add | m_sub).astype(x.dtype)
        y_add = _pipeline(x_ge, Wa, ba)
        y_sub = _pipeline(x_ge, Ws, bs)
        y = jnp.where(m_add[..., None, None], y_add, jnp.where(m_sub[..., None, None], y_sub, x_ge))
        res_lo = jnp.clip(jnp.round(y[..., 0, RESULT]), 0, 15).astype(jnp.int32)
        res_hi = jnp.clip(jnp.round(y[..., 1, RESULT]), 0, 15).astype(jnp.int32)
        oh_lo = jax.nn.one_hot(res_lo, 16, dtype=x.dtype) * active[..., None]
        oh_hi = jax.nn.one_hot(res_hi, 16, dtype=x.dtype) * active[..., None]
        carry = (jnp.round(y[..., 1, CARRY_OUT]) > 0.5).astype(x.dtype) * active
        out = x
        out = out.at[..., OUTPUT_LO:OUTPUT_LO + 16].add(2.0 * oh_lo)
        out = out.at[..., OUTPUT_HI:OUTPUT_HI + 16].add(2.0 * oh_hi)
        out = out.at[..., CARRY].add(carry)
        return out

    def _L1_attn_ref(emb, W, b):
        import jax, jax.numpy as jnp
        import numpy as np
        EMB_DIM = 128
        N_HEAD = 8
        HEAD_DIM = EMB_DIM // N_HEAD
        SEQ_LEN = 512
        BATCH = 4
        L, B, E = emb.shape
        scaling = (E / N_HEAD) ** (-0.5)
        ft = jnp.einsum('lbe,oe->lbo', emb, W) + b
        ft = ft.reshape(L, B * N_HEAD, 3 * HEAD_DIM).transpose(1, 0, 2)
        q, k, v = jnp.split(ft, 3, axis=-1)
        scores = jnp.einsum('bld,bmd->blm', q, k) * scaling
        mask = scores == 0
        scores = jnp.where(mask, -jnp.inf, scores)
        attn = jax.nn.softmax(scores, axis=-1)
        attn = jnp.where(mask, jnp.zeros((), attn.dtype), attn)
        out = jnp.einsum('blm,bmd->bld', attn, v)
        out = out.transpose(1, 0, 2).reshape(L, B, E)
        return out

    def _L1_ffn_ref(x, Wg, bg, W1, b1, W2, b2):
        import jax, jax.numpy as jnp
        import numpy as np
        B, S, D = (8, 512, 128)
        FF = 512
        E = 8
        b, s, d = x.shape
        xf = x.reshape(-1, d)
        logits = xf @ Wg + bg
        probs = jax.nn.softmax(logits, axis=-1)
        pmax = jnp.max(probs, axis=-1)
        routes = jnp.argmax(probs, axis=-1)
        xs = xf * pmax[:, None]
        out_tok = jnp.zeros_like(xf)
        for e in range(E):
            h = jax.nn.relu(xs @ W1[e] + b1[e])
            y = h @ W2[e] + b2[e]
            out_tok = jnp.where((routes == e)[:, None], y, out_tok)
        order = jnp.argsort(routes)
        return out_tok[order].reshape(b, s, d)
    h = _L0_tok_ref(x, L0_tok_kernel)
    h = h + _L0_attn_ref(_layernorm(h, axis=-1))
    h = h + _L0_ffn_ref(_layernorm(h, axis=-1), L0_ffn_Wa, L0_ffn_ba, L0_ffn_Ws, L0_ffn_bs)
    h = h + _L1_attn_ref(_layernorm(h, axis=-1), L1_attn_W, L1_attn_b)
    h = h + _L1_ffn_ref(_layernorm(h, axis=-1), L1_ffn_Wg, L1_ffn_bg, L1_ffn_W1, L1_ffn_b1, L1_ffn_W2, L1_ffn_b2)
    return h

_drawn_inputs = setup_inputs


def setup_inputs(seed=0):
    import zlib

    import numpy as np

    out = dict(_drawn_inputs(seed))
    spreads = {}
    factors = {'L1_attn_b': 2.758,
     'L1_ffn_Wg': 2.797,
     'L1_ffn_bg': 2.76,
     'L1_ffn_W1': 2.923,
     'L1_ffn_b1': 7.578,
     'L1_ffn_b2': 5.862}
    for name, (base, spread) in spreads.items():
        noise = np.random.default_rng([zlib.crc32(name.encode()), seed]).standard_normal(out[name].shape)
        drawn = base * np.exp(spread * noise) if base else spread * noise
        out[name] = jnp.asarray(drawn.astype(out[name].dtype))
    for name, factor in factors.items():
        out[name] = (out[name] * factor).astype(out[name].dtype)
    return out
```

```python
from contextlib import ExitStack

import concourse.bass as bass
from concourse import mybir

P = 128
SEQS, T_IN, D = 8, 750, 128
WINDOW = 3
T = T_IN - WINDOW + 1
HALF = T // 2
POS = -(-T // P)
TP = POS * P
T_LAST = T - (POS - 1) * P
HEADS, HD = 8, 16
QKV = 3 * D
EXPERTS, FF = 8, 512
FC = FF // P
TOKENS = SEQS * T
TILES = -(-TOKENS // P)
TOK_PAD = TILES * P
TAIL = TOKENS - (TILES - 1) * P
PAIRS = TILES + EXPERTS - 1
SLOTS = POS * SEQS
SHIFT = 64.0
EPS = 1e-5
BIG = 1e30

f32 = mybir.dt.float32
i32 = mybir.dt.int32
u32 = mybir.dt.uint32
ALU = mybir.AluOpType
ACT = mybir.ActivationFunctionType
AX = mybir.AxisListType


class Order:

    def __init__(self, eng, sem):
        self.eng, self.sem, self.base, self.n = eng, sem, 0, 0

    def link(self, ins):
        ins.then_inc(self.sem, 1)
        self.n += 1
        self.eng.wait_ge(self.sem, self.base + self.n)

    def enter(self, behind):
        self.outer, self.base, self.n = self.base + self.n, self.base + self.n + behind, 0

    def leave(self, turns, per_turn):
        assert self.n == per_turn, f"a turn has {self.n} steps, not {per_turn}"
        self.base, self.n = self.outer + turns * per_turn, 0


def moments(dve, order, stats, mean, spread, veps):
    even, odd = stats[:, :, 1], stats[:, :, 4]
    dve.tensor_tensor(mean, even, odd, ALU.add)
    dve.tensor_tensor(spread, even, odd, ALU.subtract)
    order.link(dve.tensor_tensor(veps, stats[:, :, 2], stats[:, :, 5], ALU.add))
    dve.tensor_scalar(mean, mean, 0.5, None, ALU.mult)
    dve.tensor_tensor(spread, spread, spread, ALU.mult)
    order.link(dve.tensor_scalar(veps, veps, 1.0 / D, EPS, ALU.mult, ALU.add))
    return dve.scalar_tensor_tensor(out=veps, in0=spread, scalar=0.25, in1=veps,
                                    op0=ALU.mult, op1=ALU.add)


def build(nc, xT, tok_w, qkv_w, qkv_b, gate_w, gate_b, w1, b1, w2, b2, out):
    ctx = ExitStack()
    with ctx:
        def sb(name, shape, dt=f32, scope=ctx):
            return scope.enter_context(nc.sbuf_tensor(name, shape, dt))

        def pb(name, shape, dt=f32, scope=ctx):
            return scope.enter_context(nc.psum_tensor(name, shape, dt))

        def sem(name):
            return ctx.enter_context(nc.semaphore(name))

        ident = sb("ident", [P, P])
        half_neg = sb("half_neg", [P, SEQS])
        shift_col = sb("shift_col", [P, 1])
        h_all = sb("h_all", [P, POS, SEQS, D])
        qkvw_sb = sb("qkvw_sb", [P, QKV])
        qkvb_sb = sb("qkvb_sb", [P, QKV])
        gatew_sb = sb("gatew_sb", [P, EXPERTS])
        gateb_sb = sb("gateb_sb", [P, EXPERTS])
        w1_sb = sb("w1_sb", [P, EXPERTS, FF])
        w2_sb = sb("w2_sb", [P, EXPERTS, FC, D])
        b1_sb = sb("b1_sb", [P, EXPERTS, FF])
        b2_sb = sb("b2_sb", [P, EXPERTS, D])
        onehot = sb("onehot", [P, POS, SEQS, EXPERTS])
        valid = sb("valid", [P, 1])
        before = sb("before", [P, P])
        ones = sb("ones", [P, P])

        h_dram = nc.dram_tensor("h_rows", (TOK_PAD, D), f32).ap()
        xs_dram = nc.dram_tensor("sorted_rows", (TOK_PAD, D), f32).ap()

        s_w = sem("weights_loaded")
        s_wx = sem("expert_weights_loaded")
        s_init = sem("constants_made")
        s_initg = sem("gpsimd_constants_order")
        s_dve = sem("vector_order")
        s_act = sem("scalar_order")
        s_pool = sem("gpsimd_order")
        s_pad = sem("padding_rows_zeroed")

        rows = ctx.enter_context(ExitStack())
        nT_all = sb("nT_all", [P, SEQS, TP], scope=rows)
        n_aug = sb("n_aug", [P, SEQS, POS, D + 1], scope=rows)

        with ExitStack() as a:
            x_in = [sb(f"x_in{u}", [P, T_IN], scope=a) for u in range(2)]
            tokw_sb = sb("tokw_sb", [P, WINDOW, QKV], scope=a)
            zt = [sb(f"zt{u}", [P, T], scope=a) for u in range(2)]
            ft = [sb(f"ft{u}", [P, T], scope=a) for u in range(2)]
            ot = [sb(f"ot{u}", [P, T], scope=a) for u in range(2)]
            fg = sb("forget", [P, T], scope=a)
            zin = sb("zin", [P, T], scope=a)
            cell = sb("cell", [P, T], scope=a)
            hT = [sb(f"hT{u}", [P, TP], scope=a) for u in range(2)]
            n_st = [sb(f"n_stage{u}", [P, POS, D], scope=a) for u in range(2)]
            stats = sb("stats_a", [P, POS, 6], scope=a)
            mean = sb("mean_a", [P, POS], scope=a)
            spread = sb("spread_a", [P, POS], scope=a)
            veps = sb("var_eps_a", [P, POS], scope=a)
            rstd = sb("rstd_a", [P, POS], scope=a)
            conv = pb("conv", [P, 3, 2, 512], scope=a)
            tr = pb("tr_a", [P, TP], scope=a)

            x_loaded = [sem("x_loaded_even"), sem("x_loaded_odd")]
            s_tokw = sem("conv_weights_loaded")
            conv_done, tanh_done = sem("conv_done"), sem("tanh_done")
            h_ready, hT_done, h_copied = sem("h_ready"), sem("h_transposed"), sem("h_copied")
            var_ready, rstd_ready = sem("var_ready_a"), sem("rstd_ready_a")
            n_ready, nT_done, nT_copied = sem("n_ready"), sem("n_transposed"), sem("nT_copied")
            n_kept = sem("n_kept")

            with nc.Block() as block:
                @block.sync
                def _(sp):
                    sp.dma_start(tokw_sb[:], tok_w).then_inc(s_tokw, 16)
                    for b in range(2):
                        sp.dma_start(x_in[b][:], xT[b]).then_inc(x_loaded[b], 16)
                    for dst, src in ((qkvw_sb, qkv_w), (gatew_sb, gate_w)):
                        sp.dma_start(dst[:], src).then_inc(s_w, 16)
                    sp.dma_start(qkvb_sb[:], qkv_b.partition_broadcast(P)).then_inc(s_w, 16)
                    sp.dma_start(gateb_sb[:], gate_b.partition_broadcast(P)).then_inc(s_w, 16)
                    with sp.Fori(2, SEQS - 1, 2) as b:
                        for u in range(2):
                            sp.wait_ge(conv_done, 3 * (b + u) - 3)
                            sp.dma_start(x_in[u][:], xT[bass.ds(b + u, 1)].rearrange("o p t -> (o p) t")
                                         ).then_inc(x_loaded[u], 16)
                    for dst, src in ((w1_sb, w1), (w2_sb, w2)):
                        sp.dma_start(dst[:], src).then_inc(s_wx, 16)
                    sp.dma_start(b1_sb[:], b1.partition_broadcast(P)).then_inc(s_wx, 16)
                    sp.dma_start(b2_sb[:], b2.partition_broadcast(P)).then_inc(s_wx, 16)

                @block.gpsimd
                def _(pool):
                    order = Order(pool, s_pool)
                    order.link(pool.memset(ident[:], 0.0))
                    pool.affine_select(out=ident[:], in_=ident[:], compare_op=ALU.not_equal, fill=1.0,
                                       base=0, pattern=[[-1, P]], channel_multiplier=1).then_inc(s_init, 1)
                    order.link(pool.memset(ones[:], 1.0))
                    order.link(pool.affine_select(out=before[:], in_=ones[:], compare_op=ALU.is_gt,
                                                  fill=0.0, base=0, pattern=[[1, P]],
                                                  channel_multiplier=-1))
                    order.link(pool.affine_select(out=valid[:], in_=ones[:, 0:1], compare_op=ALU.is_gt,
                                                  fill=0.0, base=T_LAST, pattern=[[0, 1]],
                                                  channel_multiplier=-1))
                    order.link(pool.memset(half_neg[:], -0.5))
                    order.link(pool.memset(shift_col[:], -SHIFT))
                    order.link(pool.memset(n_aug[:, :, :, D], 1.0))
                    for l in range(SEQS):
                        order.link(pool.tensor_copy(n_aug[:, l, POS - 1, D:D + 1], valid[:]))

                    def turn(b, u):
                        pool.wait_ge(var_ready, b + 1)
                        pool.tensor_tensor(rstd[:], veps[:], half_neg[:, 0:POS],
                                           ALU.pow).then_inc(rstd_ready, 1)
                        pool.wait_ge(n_ready, b + 1)
                        pool.tensor_copy(n_aug[:, bass.ds(b, 1), :, 0:D],
                                         n_st[u][:].rearrange("p (o j) d -> p o j d", o=1)
                                         ).then_inc(n_kept, 1)

                    with pool.Fori(0, SEQS - 1, 2) as b:
                        for u in range(2):
                            turn(b + u, u)

                @block.scalar
                def _(act):
                    def tanhs(b, u):
                        if not isinstance(b, int) or b >= 2:
                            act.wait_ge(h_ready, b - 1)
                        for g, (dst, scale) in enumerate(((zt[u], 1.0), (ft[u], 0.5), (ot[u], 0.5))):
                            act.wait_ge(conv_done, 3 * b + g + 1)
                            act.activation(dst[:].rearrange("p (h t) -> p h t", h=2),
                                           conv[:, g, :, 0:HALF], ACT.Tanh,
                                           scale=scale).then_inc(tanh_done, 1)

                    def keep_nT(b):
                        act.wait_ge(nT_done, b + 1)
                        act.activation(nT_all[:, bass.ds(b, 1), :].rearrange("p o t -> p (o t)"),
                                       tr[:], ACT.Copy).then_inc(nT_copied, 1)

                    def keep_h(b):
                        act.wait_ge(n_ready, b + 1)
                        act.activation(h_all[:, :, bass.ds(b, 1), :],
                                       tr[:].rearrange("p (j o d) -> p j o d", o=1, d=D),
                                       ACT.Copy).then_inc(h_copied, 1)

                    tanhs(0, 0)
                    tanhs(1, 1)
                    keep_h(0)
                    with act.Fori(1, SEQS - 2, 2) as b:
                        for u in range(2):
                            tanhs(b + u + 1, u)
                            keep_nT(b + u - 1)
                            keep_h(b + u)
                    keep_nT(SEQS - 2)
                    keep_h(SEQS - 1)
                    keep_nT(SEQS - 1)

                @block.vector
                def _(dve):
                    order = Order(dve, s_dve)
                    for u in range(2):
                        order.link(dve.memset(hT[u][:, T:TP], 0.0))

                    def recur(b, u):
                        dve.wait_ge(tanh_done, 3 * b + 2)
                        dve.tensor_scalar(fg[:], ft[u][:], 0.5, 0.5, ALU.mult, ALU.add)
                        order.link(dve.tensor_scalar(zin[:], ft[u][:], -0.25, 0.25, ALU.mult, ALU.add))
                        order.link(dve.tensor_tensor(zin[:], zin[:], zt[u][:], ALU.mult))
                        order.link(dve.tensor_tensor_scan(cell[:], fg[:], zin[:], 0.0,
                                                          ALU.mult, ALU.add))
                        dve.wait_ge(tanh_done, 3 * b + 3)
                        if not isinstance(b, int) or b >= 2:
                            dve.wait_ge(hT_done, b - 1)
                        dve.scalar_tensor_tensor(out=hT[u][:, 0:T], in0=ot[u][:], scalar=1.0,
                                                 in1=cell[:], op0=ALU.add,
                                                 op1=ALU.mult).then_inc(h_ready, 1)

                    def norm(b, u):
                        dve.wait_ge(hT_done, b + 1)
                        for j in range(POS):
                            last = dve.bn_stats(stats[:, j, :], tr[:, j * D:(j + 1) * D])
                        order.link(last)
                        moments(dve, order, stats, mean[:], spread[:], veps[:]).then_inc(var_ready, 1)
                        dve.wait_ge(rstd_ready, b + 1)
                        if not isinstance(b, int) or b >= 2:
                            dve.wait_ge(nT_done, b - 1)
                            dve.wait_ge(n_kept, b - 1)
                        for j in range(POS):
                            last = dve.tensor_scalar(n_st[u][:, j, :], tr[:, j * D:(j + 1) * D],
                                                     mean[:, j:j + 1], rstd[:, j:j + 1],
                                                     ALU.subtract, ALU.mult)
                        last.then_inc(n_ready, 1)

                    recur(0, 0)
                    recur(1, 1)
                    norm(0, 0)
                    recur(2, 0)
                    norm(1, 1)
                    per = 2 * 6
                    with dve.Fori(2, SEQS - 3, 2) as b:
                        order.enter((b - 2) * (per // 2))
                        for u in range(2):
                            recur(b + u + 1, 1 - u)
                            norm(b + u, u)
                    order.leave((SEQS - 4) // 2, per)
                    recur(SEQS - 1, 1)
                    norm(SEQS - 2, 0)
                    norm(SEQS - 1, 1)

                @block.tensor
                def _(pe):
                    pe.wait_ge(s_tokw, 16)
                    pe.wait_ge(s_init, 1)

                    def convolve(b, u, loaded):
                        pe.wait_ge(x_loaded[u], loaded)
                        for g in range(3):
                            if not isinstance(b, int) or b >= 1:
                                pe.wait_ge(tanh_done, 3 * b + g - 2)
                            for half in range(2):
                                for w in range(WINDOW):
                                    at = half * HALF + w
                                    last = pe.matmul(conv[:, g, half, 0:HALF],
                                                     tokw_sb[:, w, g * D:(g + 1) * D],
                                                     x_in[u][:, at:at + HALF],
                                                     start=(w == 0), stop=(w == WINDOW - 1))
                            last.then_inc(conv_done, 1)

                    def transpose_n(b, u):
                        pe.wait_ge(h_copied, b + 1)
                        for j in range(POS):
                            last = pe.transpose(tr[:, j * P:(j + 1) * P], n_st[u][:, j, :], ident[:])
                        last.then_inc(nT_done, 1)

                    def transpose_h(b, u):
                        pe.wait_ge(h_ready, b + 1)
                        if not isinstance(b, int) or b >= 1:
                            pe.wait_ge(nT_copied, b)
                        for j in range(POS):
                            last = pe.transpose(tr[:, j * P:(j + 1) * P],
                                                hT[u][:, j * P:(j + 1) * P], ident[:])
                        last.then_inc(hT_done, 1)

                    convolve(0, 0, 16)
                    convolve(1, 1, 16)
                    transpose_h(0, 0)
                    with pe.Fori(1, SEQS - 2, 2) as b:
                        for u in range(2):
                            convolve(b + u + 1, u, 8 * b + 24)
                            transpose_n(b + u - 1, u)
                            transpose_h(b + u, 1 - u)
                    transpose_n(SEQS - 2, 0)
                    transpose_h(SEQS - 1, 1)
                    transpose_n(SEQS - 1, 1)

        with ExitStack() as b_:
            expo = [sb(f"expo{u}", [P, POS, P], scope=b_) for u in range(2)]
            pv_sb = sb("pv_sb", [P, SEQS, D + 1], scope=b_)
            rec = sb("rec", [P, SEQS], scope=b_)
            hw = sb("h_work", [P, SEQS, D], scope=b_)
            nw = sb("n_work", [P, SEQS, D], scope=b_)
            h3 = sb("h3", [P, SEQS, D], scope=b_)
            n3 = sb("n3", [P, SEQS, D], scope=b_)
            nTw = sb("n_work_T", [P, SEQS, P], scope=b_)
            qkv = sb("qkv", [P, SEQS, QKV], scope=b_)
            prod = [sb(f"prod{u}", [P, HEADS, SEQS, HD], scope=b_) for u in range(2)]
            scores = sb("scores", [P, SEQS, HEADS, SEQS], scope=b_)
            notmask = sb("notmask", [P, SEQS, HEADS, SEQS], scope=b_)
            probs = sb("probs", [P, SEQS, HEADS, SEQS], scope=b_)
            top = sb("top", [P, SEQS, HEADS], scope=b_)
            att = sb("att", [P, SEQS, D], scope=b_)
            statsb = sb("stats_b", [P, SEQS, 6], scope=b_)
            meanb = sb("mean_b", [P, SEQS], scope=b_)
            spreadb = sb("spread_b", [P, SEQS], scope=b_)
            vepsb = sb("var_eps_b", [P, SEQS], scope=b_)
            rstdb = sb("rstd_b", [P, SEQS], scope=b_)
            logit = sb("logit", [P, SEQS, EXPERTS], scope=b_)
            elog = sb("exp_logit", [P, SEQS, EXPERTS], scope=b_)
            mxl = sb("max_logit", [P, SEQS], scope=b_)
            best = sb("best", [P, SEQS, EXPERTS], scope=b_)
            firstw = sb("first_weight", [P, EXPERTS], scope=b_)
            s_ps = [pb(f"scores_ps{u}", [P, 1024], scope=b_) for u in range(2)]
            pv_ps = [pb(f"pv_ps{u}", [P, 512], scope=b_) for u in range(2)]
            t_ps = pb("t_ps", [P, 512], scope=b_)
            q_ps = pb("q_ps", [P, 512], scope=b_)

            s_dveb = sem("vector_order_b")
            s_done, exp_done = sem("nn_done"), sem("exp_done")
            pv_done, pv_copied, pv_read = sem("pv_done"), sem("pv_copied"), sem("pv_read")
            varb_ready, rstdb_ready = sem("var_ready_b"), sem("rstd_ready_b")
            n2_ready, n3_ready = sem("n2_ready"), sem("n3_ready")
            t_done, t_copied = sem("t_done"), sem("t_copied")
            q_done, q_read = sem("qkv_done"), sem("qkv_read")
            g_done, g_read = sem("gate_done"), sem("gate_read")
            sm_ready, sm_done = sem("head_scores_ready"), sem("head_exp_done")
            probs_ready, av_ready, av_read = sem("probs_ready"), sem("av_ready"), sem("av_read")
            h3_ready, h3_stored = sem("h3_ready"), sem("h3_stored")
            lg_ready, lg_done = sem("logits_ready"), sem("logits_exp_done")

            def known(v):
                return isinstance(v, int)

            def at(v):
                return bass.ds(v, 1)

            def t_before_project(i):
                return 4 * i

            def t_before_gate(i):
                return 4 * i + 2

            def schedule(turn, loop):
                turn(0)
                turn(1)
                with loop(2, POS) as it:
                    turn(it)
                turn(POS)
                turn(POS + 1)

            with nc.Block() as block:
                @block.tensor
                def _(pe):
                    def self_attention(i):
                        def nn(l):
                            if not (known(i) and i == 0 and l < 2):
                                pe.wait_ge(exp_done, SEQS * i + l - 1)
                            for j in range(POS):
                                last = pe.matmul(s_ps[l % 2][:, j * P:(j + 1) * P],
                                                 nT_all[:, l, j * P:(j + 1) * P],
                                                 nT_all[:, l, bass.ds(i * P, P)], start=True, stop=True)
                            last.then_inc(s_done, 1)

                        def pv(l):
                            pe.wait_ge(exp_done, SEQS * i + l + 1)
                            if not (known(i) and i == 0 and l < 2):
                                pe.wait_ge(pv_copied, SEQS * i + l - 1)
                            for j in range(POS):
                                last = pe.matmul(pv_ps[l % 2][:, 0:D + 1], expo[l % 2][:, j, :],
                                                 n_aug[:, l, j, :], start=(j == 0), stop=(j == POS - 1))
                            last.then_inc(pv_done, 1)

                        nn(0)
                        for l in range(1, SEQS):
                            nn(l)
                            pv(l - 1)
                        pv(SEQS - 1)

                    def transpose_4(src, group, t_before):
                        if not known(t_before) or t_before + group > 0:
                            pe.wait_ge(t_copied, t_before + group)
                        for m in range(4):
                            last = pe.transpose(t_ps[:, m * P:(m + 1) * P], src[:, 4 * group + m, :],
                                                ident[:])
                        last.then_inc(t_done, 1)

                    def gate(i):
                        pe.wait_ge(n3_ready, i + 1)
                        for group in range(2):
                            transpose_4(n3, group, t_before_gate(i))
                        pe.wait_ge(t_copied, t_before_gate(i) + 2)
                        pe.wait_ge(q_read, SEQS * (i + 1))
                        for l in range(SEQS):
                            last = pe.matmul(q_ps[:, l * EXPERTS:(l + 1) * EXPERTS], nTw[:, l, :],
                                             gatew_sb[:], start=True, stop=True)
                        last.then_inc(g_done, 1)

                    def project(i):
                        pe.wait_ge(n2_ready, i + 1)
                        for group in range(2):
                            transpose_4(nw, group, t_before_project(i))
                        pe.wait_ge(t_copied, t_before_project(i) + 2)
                        if not known(i) or i >= 1:
                            pe.wait_ge(g_read, i)
                        for l in range(SEQS):
                            if l:
                                pe.wait_ge(q_read, SEQS * i + l)
                            pe.matmul(q_ps[:, 0:QKV], nTw[:, l, :], qkvw_sb[:],
                                      start=True, stop=True).then_inc(q_done, 1)

                    def turn(it):
                        if not known(it) or it < POS:
                            self_attention(it)
                        if not known(it) or it >= 2:
                            gate(it - 2)
                        if not known(it) or 1 <= it <= POS:
                            project(it - 1)

                    schedule(turn, pe.Fori)

                @block.scalar
                def _(act):
                    def copy_t(t_before, group):
                        act.wait_ge(t_done, t_before + group + 1)
                        act.activation(nTw[:, 4 * group:4 * group + 4, :].rearrange("p a b -> p (a b)"),
                                       t_ps[:], ACT.Copy).then_inc(t_copied, 1)

                    def turn(it):
                        if not known(it) or it < POS:
                            for l in range(SEQS + 1):
                                if l < SEQS:
                                    act.wait_ge(s_done, SEQS * it + l + 1)
                                    if not known(it) or SEQS * it + l >= 2:
                                        act.wait_ge(pv_done, SEQS * it + l - 1)
                                    act.activation(expo[l % 2][:].rearrange("p a b -> p (a b)"),
                                                   s_ps[l % 2][:, 0:TP], ACT.Exp,
                                                   bias=shift_col[:]).then_inc(exp_done, 1)
                                if l == 1 and (not known(it) or it >= 1):
                                    act.wait_ge(pv_read, it)
                                if l >= 1:
                                    act.wait_ge(pv_done, SEQS * it + l)
                                    act.activation(pv_sb[:, l - 1, :], pv_ps[(l - 1) % 2][:, 0:D + 1],
                                                   ACT.Copy).then_inc(pv_copied, 1)
                        if not known(it) or it >= 2:
                            i = it - 2
                            act.wait_ge(q_done, SEQS * (i + 1))
                            for group in range(2):
                                copy_t(t_before_gate(i), group)
                            act.wait_ge(lg_ready, i + 1)
                            act.activation(elog[:], logit[:], ACT.Exp).then_inc(lg_done, 1)
                        if not known(it) or 1 <= it <= POS:
                            i = it - 1
                            if not known(i) or i >= 1:
                                act.wait_ge(g_done, i)
                            for group in range(2):
                                copy_t(t_before_project(i), group)
                            act.wait_ge(sm_ready, i + 1)
                            act.activation(probs[:], probs[:], ACT.Exp).then_inc(sm_done, 1)

                    schedule(turn, act.Fori)

                @block.gpsimd
                def _(pool):
                    def rstd_of(n):
                        pool.wait_ge(varb_ready, n)
                        pool.tensor_tensor(rstdb[:], vepsb[:], half_neg[:], ALU.pow
                                           ).then_inc(rstdb_ready, 1)

                    def turn(i):
                        rstd_of(3 * i + 1)
                        rstd_of(3 * i + 2)
                        pool.wait_ge(probs_ready, i + 1)
                        for l in range(SEQS):
                            if not known(i) or SEQS * i + l >= 2:
                                pool.wait_ge(av_read, SEQS * i + l - 1)
                            pool.tensor_tensor(
                                prod[l % 2][:],
                                probs[:, l, :, :].unsqueeze(3).broadcast_to([P, HEADS, SEQS, HD]),
                                value_rows, ALU.mult).then_inc(av_ready, 1)
                        rstd_of(3 * i + 3)

                    value_rows = qkv[:].rearrange("p m (h c) -> p h m c", c=3 * HD)[:, :, :, 2 * HD:3 * HD]
                    turn(0)
                    with pool.Fori(1, POS) as i:
                        turn(i)

                @block.sync
                def _(sp):
                    rows_of = h_dram[0:TOKENS].rearrange("(l t) d -> t l d", l=SEQS)
                    with sp.Fori(0, POS - 1) as i:
                        sp.wait_ge(h3_ready, i + 1)
                        sp.dma_start(rows_of[bass.ds(i * P, P)], h3[:]).then_inc(h3_stored, 16)
                    sp.wait_ge(h3_ready, POS)
                    sp.dma_start(rows_of[(POS - 1) * P:T], h3[0:T_LAST]).then_inc(h3_stored, 16)

                @block.vector
                def _(dve):
                    order = Order(dve, s_dveb)
                    for e in range(EXPERTS):
                        last = dve.memset(firstw[:, e:e + 1], float(EXPERTS - e))
                    order.link(last)
                    dve.wait_ge(s_w, 64)

                    def wide(col, n):
                        return col.unsqueeze(2).broadcast_to([P, SEQS, n])

                    def layernorm(src, dst, n):
                        for l in range(SEQS):
                            last = dve.bn_stats(statsb[:, l, :], src[:, l, :])
                        order.link(last)
                        moments(dve, order, statsb, meanb[:], spreadb[:], vepsb[:]
                                ).then_inc(varb_ready, 1)
                        dve.wait_ge(rstdb_ready, n)
                        for l in range(SEQS):
                            last = dve.tensor_scalar(dst[:, l, :], src[:, l, :], meanb[:, l:l + 1],
                                                     rstdb[:, l:l + 1], ALU.subtract, ALU.mult)
                        return last

                    def residuals(i):
                        dve.wait_ge(pv_copied, SEQS * (i + 1))
                        order.link(dve.reciprocal(rec[:], pv_sb[:, :, D]))
                        dve.tensor_tensor(hw[:], pv_sb[:, :, 0:D], wide(rec[:], D),
                                          ALU.mult).then_inc(pv_read, 1)
                        dve.wait_ge(pv_read, i + 1)
                        order.link(dve.tensor_tensor(hw[:], hw[:], n_aug[:, :, at(i), 0:D].rearrange(
                            "p l o d -> p (l o) d"), ALU.mult))
                        order.link(dve.tensor_tensor(hw[:], hw[:], h_all[:, at(i)].rearrange(
                            "p o l d -> p (o l) d"), ALU.add))
                        if not known(i) or i >= 1:
                            dve.wait_ge(t_done, t_before_project(i - 1) + 2)
                        order.link(layernorm(hw, nw, 3 * i + 1))
                        order.link(dve.tensor_tensor(hw[:], hw[:], nw[:], ALU.add))
                        layernorm(hw, nw, 3 * i + 2).then_inc(n2_ready, 1)

                    def head_attention(i):
                        for l in range(SEQS):
                            dve.wait_ge(q_done, SEQS * i + l + 1)
                            dve.tensor_tensor(qkv[:, l, :], q_ps[:, 0:QKV], qkvb_sb[:],
                                              ALU.add).then_inc(q_read, 1)
                        dve.wait_ge(q_read, SEQS * (i + 1))
                        heads = qkv[:].rearrange("p m (h c) -> p h m c", c=3 * HD)
                        for l in range(SEQS):
                            query = heads[:, :, l, 0:HD].unsqueeze(2).broadcast_to([P, HEADS, SEQS, HD])
                            order.link(dve.tensor_tensor(prod[l % 2][:], query,
                                                         heads[:, :, :, HD:2 * HD], ALU.mult))
                            last = dve.tensor_reduce(scores[:, l], prod[l % 2][:], AX.X, ALU.add)
                        order.link(last)
                        flat = "p l h m -> p (l h) m"
                        sc, nm, pr = (x[:].rearrange(flat) for x in (scores, notmask, probs))
                        tp = top[:].rearrange("p l h -> p (l h)")
                        tpw = tp.unsqueeze(2).broadcast_to([P, SEQS * HEADS, SEQS])
                        order.link(dve.tensor_scalar(nm, sc, HD ** -0.5, 0.0, ALU.mult, ALU.not_equal))
                        order.link(dve.tensor_scalar(pr, nm, BIG, -BIG, ALU.mult, ALU.add))
                        order.link(dve.scalar_tensor_tensor(out=pr, in0=sc, scalar=HD ** -0.5, in1=pr,
                                                            op0=ALU.mult, op1=ALU.add))
                        order.link(dve.tensor_reduce(tp, pr, AX.X, ALU.max))
                        dve.tensor_tensor(pr, pr, tpw, ALU.subtract).then_inc(sm_ready, 1)
                        dve.wait_ge(sm_done, i + 1)
                        order.link(dve.tensor_tensor(pr, pr, nm, ALU.mult))
                        order.link(dve.tensor_reduce(tp, pr, AX.X, ALU.add))
                        order.link(dve.tensor_scalar(tp, tp, 1.0 / BIG, None, ALU.max))
                        order.link(dve.reciprocal(tp, tp))
                        dve.tensor_tensor(pr, pr, tpw, ALU.mult).then_inc(probs_ready, 1)
                        for l in range(SEQS):
                            dve.wait_ge(av_ready, SEQS * i + l + 1)
                            dve.tensor_reduce(att[:, l, :].rearrange("p (h c) -> p h c", c=HD),
                                              prod[l % 2][:].rearrange("p h m c -> p h c m"),
                                              AX.X, ALU.add).then_inc(av_read, 1)
                        dve.wait_ge(av_read, SEQS * (i + 1))
                        if not known(i) or i >= 1:
                            dve.wait_ge(h3_stored, 16 * i)
                        dve.tensor_tensor(h3[:], hw[:], att[:], ALU.add).then_inc(h3_ready, 1)
                        dve.wait_ge(h3_ready, i + 1)
                        layernorm(h3, n3, 3 * i + 3).then_inc(n3_ready, 1)

                    def route(i):
                        dve.wait_ge(g_done, i + 1)
                        dve.tensor_tensor(
                            logit[:], q_ps[:, 0:SEQS * EXPERTS].rearrange("p (l e) -> p l e", e=EXPERTS),
                            gateb_sb[:].unsqueeze(1).broadcast_to([P, SEQS, EXPERTS]),
                            ALU.add).then_inc(g_read, 1)
                        dve.wait_ge(g_read, i + 1)
                        oh = onehot[:, at(i)].rearrange("p o l e -> p (o l) e")
                        order.link(dve.tensor_reduce(mxl[:], logit[:], AX.X, ALU.max))
                        order.link(dve.tensor_tensor(best[:], logit[:], wide(mxl[:], EXPERTS),
                                                     ALU.is_equal))
                        dve.tensor_tensor(logit[:], logit[:], wide(mxl[:], EXPERTS),
                                          ALU.subtract).then_inc(lg_ready, 1)
                        order.link(dve.tensor_tensor(
                            best[:], best[:], firstw[:].unsqueeze(1).broadcast_to([P, SEQS, EXPERTS]),
                            ALU.mult))
                        order.link(dve.tensor_reduce(mxl[:], best[:], AX.X, ALU.max))
                        order.link(dve.tensor_tensor(oh, best[:], wide(mxl[:], EXPERTS), ALU.is_equal))
                        if known(i) and i == POS - 1:
                            dve.tensor_scalar(oh, oh, valid[:], None, ALU.mult)
                        dve.wait_ge(lg_done, i + 1)
                        order.link(dve.tensor_reduce(mxl[:], elog[:], AX.X, ALU.add))
                        order.link(dve.reciprocal(mxl[:], mxl[:]))
                        order.link(dve.tensor_tensor(h_all[:, at(i)].rearrange("p o l d -> p (o l) d"),
                                                     n3[:], wide(mxl[:], D), ALU.mult))

                    residuals(0)
                    head_attention(0)
                    per = 39
                    with dve.Fori(1, POS) as i:
                        order.enter((i - 1) * per)
                        residuals(i)
                        route(i - 1)
                        head_attention(i)
                    order.leave(POS - 1, per)
                    route(POS - 1)
        rows.close()
        place = sb("place", [P, POS, SEQS], u32)
        tile_of = sb("tile_of", [P, PAIRS], i32)
        expert_of = sb("expert_of", [P, PAIRS], i32)
        owned = sb("owned", [P, PAIRS])
        with ExitStack() as c_:
            total = sb("total", [P, EXPERTS, SEQS, POS], scope=c_)
            upto = sb("upto", [P, EXPERTS, SEQS, POS], scope=c_)
            below = sb("below", [P, EXPERTS, SEQS, POS], scope=c_)
            ones_row = sb("ones_row", [P, EXPERTS * SLOTS], scope=c_)
            spot = sb("spot", [P, POS, SEQS, EXPERTS], scope=c_)
            placef = sb("placef", [P, SLOTS], scope=c_)
            ints = sb("ints", [P, PAIRS + TILES + EXPERTS + 1], i32, scope=c_)
            nums = sb("nums", [P, PAIRS + TILES + EXPERTS + 1], scope=c_)
            q_row = nums[:, 0:PAIRS]
            cut_row = nums[:, PAIRS + 1:PAIRS + TILES]
            e_row = nums[:, PAIRS + TILES:PAIRS + TILES + EXPERTS]
            p_col = nums[:, PAIRS + TILES + EXPERTS:]
            ends = sb("ends", [P, 4, EXPERTS], scope=c_)
            start, stop, jump, last_tile = (ends[:, n, :] for n in range(4))
            count = sb("pair_count", [P, EXPERTS], scope=c_)
            cincl = sb("pairs_upto", [P, EXPERTS], scope=c_)
            cuts = sb("cuts", [P, EXPERTS, TILES - 1], scope=c_)
            sel = sb("sel", [P, PAIRS, EXPERTS], scope=c_)
            tmp = sb("sel_times", [P, PAIRS, EXPERTS], scope=c_)
            expf = sb("expert_f", [P, PAIRS], scope=c_)
            tilef = sb("tile_f", [P, PAIRS], scope=c_)
            first_row = sb("first_row", [P, PAIRS], scope=c_)
            stop_row = sb("stop_row", [P, PAIRS], scope=c_)
            row = sb("row", [P, PAIRS], scope=c_)
            zeros = sb("zeros", [TOK_PAD - TOKENS, D], scope=c_)
            before_ps = pb("before_ps", [P, 512], scope=c_)
            total_ps = pb("total_ps", [P, 512], scope=c_)
            s_cnt, s_rows, s_place = sem("counted"), sem("index_rows_made"), sem("places_ready")
            s_scat, s_dvec = sem("rows_scattered"), sem("vector_order_c")
            s_zero = sem("zeros_made")

            with nc.Block() as block:
                @block.tensor
                def _(pe):
                    flat = onehot[:].rearrange("p i l e -> p (i l e)")
                    pe.matmul(before_ps[:, 0:SLOTS * EXPERTS], before[:], flat, start=True, stop=True)
                    pe.matmul(total_ps[:, 0:SLOTS * EXPERTS], ones[:], flat,
                              start=True, stop=True).then_inc(s_cnt, 1)

                @block.gpsimd
                def _(pool):
                    pool.memset(zeros[:], 0.0).then_inc(s_zero, 1)
                    for at0, n, step, chan in ((0, PAIRS, 1, 0), (PAIRS, TILES, P, 0),
                                               (PAIRS + TILES, EXPERTS, 1, 0),
                                               (PAIRS + TILES + EXPERTS, 1, 0, 1)):
                        pool.iota(ints[:, at0:at0 + n], pattern=[[step, n]], base=0,
                                  channel_multiplier=chan).then_inc(s_rows, 1)
                    pool.wait_ge(s_place, 1)
                    for i in range(POS):
                        for l in range(SEQS):
                            n = T_LAST if i == POS - 1 else P
                            pool.indirect_dma_start(
                                xs_dram[0:TOKENS, :],
                                bass.IndirectOffsetOnAxis(ap=place[0:n, i, l:l + 1], axis=0),
                                h_all[0:n, i, l, :], None,
                                bounds_check=TOKENS - 1, oob_is_err=False).then_inc(s_scat, 16)
                    pool.wait_ge(s_scat, 16 * SLOTS)

                @block.sync
                def _(sp):
                    sp.wait_ge(s_zero, 1)
                    for dst in (xs_dram, h_dram):
                        sp.dma_start(dst[TOKENS:TOK_PAD], zeros[:]).then_inc(s_pad, 16)
                    sp.wait_ge(s_pad, 32)

                @block.vector
                def _(dve):
                    order = Order(dve, s_dvec)
                    order.link(dve.memset(ones_row[:], 1.0))
                    dve.wait_ge(s_cnt, 1)
                    order.link(dve.tensor_copy(total[:], total_ps[:, 0:SLOTS * EXPERTS].rearrange(
                        "p (i l e) -> p e l i", i=POS, l=SEQS)))
                    run = "p e l i -> p (e l i)"
                    order.link(dve.tensor_tensor_scan(upto[:].rearrange(run), ones_row[:],
                                                      total[:].rearrange(run), 0.0, ALU.mult, ALU.add))
                    order.link(dve.tensor_tensor(below[:].rearrange(run), upto[:].rearrange(run),
                                                 total[:].rearrange(run), ALU.subtract))
                    for e in range(EXPERTS):
                        last = dve.tensor_tensor(
                            spot[:, :, :, e],
                            before_ps[:, 0:SLOTS * EXPERTS].rearrange("p (i l e) -> p i l e", i=POS,
                                                                      l=SEQS)[:, :, :, e],
                            below[:, e].rearrange("p l i -> p i l"), ALU.add)
                    order.link(last)
                    order.link(dve.tensor_tensor(spot[:], spot[:], onehot[:], ALU.mult))
                    order.link(dve.tensor_reduce(placef[:], spot[:].rearrange("p i l e -> p (i l) e"),
                                                 AX.X, ALU.add))
                    dve.tensor_copy(place[:].rearrange("p i l -> p (i l)"),
                                    placef[:]).then_inc(s_place, 1)

                    dve.wait_ge(s_rows, 4)
                    dve.tensor_copy(nums[:], ints[:])
                    dve.tensor_copy(start, below[:, :, 0, 0])
                    order.link(dve.tensor_copy(stop, upto[:, :, SEQS - 1, POS - 1]))

                    def tiles_before(dst, bound, compare):
                        cut = cut_row.unsqueeze(1).broadcast_to([P, EXPERTS, TILES - 1])
                        order.link(dve.tensor_tensor(
                            cuts[:], bound.unsqueeze(2).broadcast_to([P, EXPERTS, TILES - 1]), cut,
                            compare))
                        order.link(dve.tensor_reduce(dst, cuts[:], AX.X, ALU.add))

                    tiles_before(jump, start, ALU.is_ge)
                    tiles_before(last_tile, stop, ALU.is_gt)
                    order.link(dve.tensor_tensor(count[:], last_tile, jump, ALU.subtract))
                    dve.tensor_tensor(last_tile, stop, start, ALU.is_gt)
                    order.link(dve.tensor_scalar(count[:], count[:], 1.0, None, ALU.add))
                    order.link(dve.tensor_tensor(count[:], count[:], last_tile, ALU.mult))
                    order.link(dve.tensor_tensor_scan(cincl[:], ones_row[:, 0:EXPERTS], count[:], 0.0,
                                                      ALU.mult, ALU.add))
                    order.link(dve.tensor_tensor(count[:], cincl[:], count[:], ALU.subtract))
                    order.link(dve.tensor_tensor(jump, jump, count[:], ALU.subtract))

                    def by_pair(v):
                        return v.unsqueeze(2).broadcast_to([P, PAIRS, EXPERTS])

                    def by_expert(v):
                        return v.unsqueeze(1).broadcast_to([P, PAIRS, EXPERTS])

                    order.link(dve.tensor_tensor(tmp[:], by_pair(q_row), by_expert(cincl[:]), ALU.is_ge))
                    order.link(dve.tensor_reduce(expf[:], tmp[:], AX.X, ALU.add))
                    order.link(dve.tensor_scalar(expf[:], expf[:], EXPERTS - 1.0, None, ALU.min))
                    order.link(dve.tensor_tensor(sel[:], by_pair(expf[:]), by_expert(e_row),
                                                 ALU.is_equal))
                    dve.tensor_copy(expert_of[:], expf[:])
                    for dst, src in ((tilef, jump), (first_row, start), (stop_row, stop)):
                        order.link(dve.tensor_tensor(tmp[:], sel[:], by_expert(src), ALU.mult))
                        order.link(dve.tensor_reduce(dst[:], tmp[:], AX.X, ALU.add))
                    order.link(dve.tensor_tensor(tilef[:], tilef[:], q_row, ALU.add))
                    order.link(dve.tensor_scalar(tilef[:], tilef[:], TILES - 1.0, None, ALU.min))
                    dve.tensor_copy(tile_of[:], tilef[:])
                    order.link(dve.tensor_scalar(row[:], tilef[:], float(P), p_col, ALU.mult, ALU.add))
                    dve.tensor_tensor(first_row[:], row[:], first_row[:], ALU.is_ge)
                    order.link(dve.tensor_tensor(stop_row[:], row[:], stop_row[:], ALU.is_lt))
                    order.link(dve.tensor_tensor(first_row[:], first_row[:], stop_row[:], ALU.mult))
                    order.link(dve.tensor_scalar(row[:], q_row, cincl[:, EXPERTS - 1:], None, ALU.is_lt))
                    order.link(dve.tensor_tensor(owned[:], first_row[:], row[:], ALU.mult))

        with ExitStack() as d_:
            y = sb("y", [P, TILES, D], scope=d_)
            x_rows = [sb(f"x_rows{u}", [P, D], scope=d_) for u in range(2)]
            xTd = [sb(f"xT_sorted{u}", [P, P], scope=d_) for u in range(2)]
            hid = [sb(f"hidden{u}", [P, FF], scope=d_) for u in range(2)]
            hidT = [sb(f"hidden_T{u}", [P, FC, P], scope=d_) for u in range(2)]
            yb = sb("y_bias", [P, D], scope=d_)
            x_ps = pb("x_ps", [P, 512], scope=d_)
            hid_ps = [pb(f"hid_ps{u}", [P, FF], scope=d_) for u in range(2)]
            hT_ps = [pb(f"hT_ps{u}", [P, 512], scope=d_) for u in range(2)]
            y_ps = [pb(f"y_ps{u}", [P, 512], scope=d_) for u in range(2)]
            y_loaded, s_out = sem("h_rows_loaded"), sem("out_stored")
            rows_in = [sem("rows_in_even"), sem("rows_in_odd")]
            x_done, xT_ready = sem("x_transposed"), sem("xT_ready")
            up_done, hid_ready = sem("up_done"), sem("hidden_ready")
            hT_done2, hidT_ready = sem("hidden_transposed"), sem("hidden_T_ready")
            down_done, y_read, y_added = sem("down_done"), sem("y_read"), sem("y_added")
            LAG = EXPERTS
            END = PAIRS + 3

            def steps(step, loop, first=4):
                for t in range(first):
                    step(t, t % 2)
                with loop(first, PAIRS - 1, 2) as t:
                    for u in range(2):
                        step(t + u, u)
                for t in range(PAIRS, END):
                    step(t, t % 2)

            def is_int(v):
                return isinstance(v, int)

            with nc.Block() as block:
                @block.sync
                def _(sp):
                    out_tiles = out[0:(TILES - 1) * P].rearrange("(k p) d -> p k d", p=P)
                    h_tiles = h_dram.rearrange("(k p) d -> p k d", p=P)
                    x_tiles = xs_dram.rearrange("(k p) d -> k p d", p=P)

                    def load(t, u):
                        if not is_int(t) or t >= 2:
                            sp.wait_ge(x_done, t - 1)
                        k = sp.value_load(tile_of[0:1, bass.ds(t, 1)], min_val=0, max_val=TILES - 1)
                        sp.dma_start(x_rows[u][:], x_tiles[bass.ds(k, 1)].rearrange("o p d -> (o p) d")
                                     ).then_inc(rows_in[u], 16)

                    def store(q):
                        sp.wait_ge(y_added, q + 1)
                        k = q - LAG
                        sp.dma_start(out_tiles[:, bass.ds(k, 1), :],
                                     y[:, bass.ds(k, 1), :]).then_inc(s_out, 16)

                    load(0, 0)
                    load(1, 1)
                    sp.wait_ge(h3_stored, 16 * POS)
                    sp.dma_start(y[:], h_tiles).then_inc(y_loaded, 16)
                    with sp.Fori(2, LAG + 3, 2) as t:
                        for u in range(2):
                            load(t + u, u)
                    with sp.Fori(LAG + 4, PAIRS - 1, 2) as t:
                        for u in range(2):
                            load(t + u, u)
                            store(t + u - 4)
                    for q in range(PAIRS - 4, PAIRS):
                        store(q)
                    sp.dma_start(out[(TILES - 1) * P:TOKENS], y[0:TAIL, TILES - 1, :]).then_inc(s_out, 16)
                    sp.wait_ge(s_out, 16 * TILES)

                @block.tensor
                def _(pe):
                    def step(t, u):
                        v = 1 - u
                        if not is_int(t) or t < PAIRS:
                            pe.wait_ge(rows_in[u], 8 * (t - u) + 16)
                            if not is_int(t) or t >= 1:
                                pe.wait_ge(xT_ready, t)
                            pe.transpose(x_ps[:, 0:P], x_rows[u][:], ident[:]).then_inc(x_done, 1)
                        if not is_int(t) or 1 <= t <= PAIRS:
                            pe.wait_ge(xT_ready, t)
                            if not is_int(t) or t >= 3:
                                pe.wait_ge(hid_ready, t - 2)
                            e = pe.value_load(expert_of[0:1, bass.ds(t - 1, 1)], min_val=0,
                                              max_val=EXPERTS - 1)
                            pe.matmul(hid_ps[v][:], xTd[v][:],
                                      w1_sb[:, bass.ds(e, 1), :].rearrange("p o f -> p (o f)"),
                                      start=True, stop=True).then_inc(up_done, 1)
                        if not is_int(t) or 2 <= t <= PAIRS + 1:
                            pe.wait_ge(hid_ready, t - 1)
                            if not is_int(t) or t >= 4:
                                pe.wait_ge(hidT_ready, t - 3)
                            for c in range(FC):
                                last = pe.transpose(hT_ps[u][:, c * P:(c + 1) * P],
                                                    hid[u][:, c * P:(c + 1) * P], ident[:])
                            last.then_inc(hT_done2, 1)
                        if not is_int(t) or t >= 3:
                            pe.wait_ge(hidT_ready, t - 2)
                            if not is_int(t) or t >= 5:
                                pe.wait_ge(y_read, t - 4)
                            e = pe.value_load(expert_of[0:1, bass.ds(t - 3, 1)], min_val=0,
                                              max_val=EXPERTS - 1)
                            for c in range(FC):
                                last = pe.matmul(y_ps[v][:, 0:D], hidT[v][:, c, :],
                                                 w2_sb[:, bass.ds(e, 1), c, :].rearrange(
                                                     "p o d -> p (o d)"),
                                                 start=(c == 0), stop=(c == FC - 1))
                            last.then_inc(down_done, 1)

                    pe.wait_ge(s_wx, 64)
                    steps(step, pe.Fori, 6)

                @block.scalar
                def _(act):
                    def step(t, u):
                        if not is_int(t) or t < PAIRS:
                            act.wait_ge(x_done, t + 1)
                            if not is_int(t) or t >= 2:
                                act.wait_ge(up_done, t - 1)
                            act.activation(xTd[u][:], x_ps[:, 0:P], ACT.Copy).then_inc(xT_ready, 1)
                        if not is_int(t) or 2 <= t <= PAIRS + 1:
                            act.wait_ge(hT_done2, t - 1)
                            if not is_int(t) or t >= 4:
                                act.wait_ge(down_done, t - 3)
                            act.activation(hidT[u][:].rearrange("p c t -> p (c t)"), hT_ps[u][:],
                                           ACT.Relu).then_inc(hidT_ready, 1)

                    steps(step, act.Fori, 6)

                @block.vector
                def _(dve):
                    def step(t, u):
                        v = 1 - u
                        if not is_int(t) or 1 <= t <= PAIRS:
                            dve.wait_ge(up_done, t)
                            if not is_int(t) or t >= 3:
                                dve.wait_ge(hT_done2, t - 2)
                            e = dve.value_load(expert_of[0:1, bass.ds(t - 1, 1)], min_val=0,
                                               max_val=EXPERTS - 1)
                            dve.tensor_tensor(hid[v][:], hid_ps[v][:],
                                              b1_sb[:, bass.ds(e, 1), :].rearrange("p o f -> p (o f)"),
                                              ALU.add).then_inc(hid_ready, 1)
                        if not is_int(t) or t >= 3:
                            dve.wait_ge(down_done, t - 2)
                            if not is_int(t) or t >= 4:
                                dve.wait_ge(y_added, t - 3)
                            e = dve.value_load(expert_of[0:1, bass.ds(t - 3, 1)], min_val=0,
                                               max_val=EXPERTS - 1)
                            k = dve.value_load(tile_of[0:1, bass.ds(t - 3, 1)], min_val=0,
                                               max_val=TILES - 1)
                            dve.tensor_tensor(yb[:], y_ps[v][:, 0:D],
                                              b2_sb[:, bass.ds(e, 1), :].rearrange("p o d -> p (o d)"),
                                              ALU.add).then_inc(y_read, 1)
                            dve.wait_ge(y_read, t - 2)
                            y_tile = y[:, bass.ds(k, 1), :].rearrange("p o d -> p (o d)")
                            dve.scalar_tensor_tensor(out=y_tile, in0=yb[:],
                                                     scalar=owned[:, bass.ds(t - 3, 1)], in1=y_tile,
                                                     op0=ALU.mult, op1=ALU.add).then_inc(y_added, 1)

                    dve.wait_ge(s_wx, 64)
                    dve.wait_ge(y_loaded, 16)
                    steps(step, dve.Fori, 6)


def kernel(x, L0_tok_kernel, L0_ffn_Wa, L0_ffn_ba, L0_ffn_Ws, L0_ffn_bs, L1_attn_W, L1_attn_b,
           L1_ffn_Wg, L1_ffn_bg, L1_ffn_W1, L1_ffn_b1, L1_ffn_W2, L1_ffn_b2):
    import numpy as _np
    import concourse.bacc as _bacc
    from concourse import mybir as _mybir
    from concourse.bass_utils import run_bass_kernel_spmd as _run

    nc = _bacc.Bacc("TRN2", target_bir_lowering=False, num_devices=1)
    laid_out = {
        "xT": _np.asarray(x).transpose(0, 2, 1),
        "tok_w": _np.asarray(L0_tok_kernel).transpose(1, 0, 2),
        "qkv_w": _np.asarray(L1_attn_W).T,
        "qkv_b": _np.asarray(L1_attn_b),
        "gate_w": _np.asarray(L1_ffn_Wg),
        "gate_b": _np.asarray(L1_ffn_bg),
        "w1": _np.asarray(L1_ffn_W1).transpose(1, 0, 2),
        "b1": _np.asarray(L1_ffn_b1),
        "w2": _np.asarray(L1_ffn_W2).reshape(EXPERTS, FC, P, D).transpose(2, 0, 1, 3),
        "b2": _np.asarray(L1_ffn_b2),
    }
    arrays, args = {}, []
    for name, a in laid_out.items():
        a = _np.ascontiguousarray(a)
        arrays[name] = a
        args.append(nc.dram_tensor(name, a.shape, _mybir.dt.from_np(a.dtype), kind="ExternalInput").ap())
    args.append(nc.dram_tensor("out", (TOKENS, D), _mybir.dt.float32, kind="ExternalOutput").ap())
    build(nc, *args)
    r = _run(nc, [arrays], core_ids=[0])
    return r.results[0]["out"].reshape(SEQS, T, D)
```

```python
from contextlib import ExitStack

import concourse.bass as bass
from concourse import mybir

P = 128
SEQS, T_IN, D = 8, 750, 128
WINDOW = 3
T = T_IN - WINDOW + 1
HALF = T // 2
POS = -(-T // P)
TP = POS * P
T_LAST = T - (POS - 1) * P
HEADS, HD = 8, 16
QKV = 3 * D
EXPERTS, FF = 8, 512
FC = FF // P
TOKENS = SEQS * T
TILES = -(-TOKENS // P)
TOK_PAD = TILES * P
TAIL = TOKENS - (TILES - 1) * P
PAIRS = TILES + EXPERTS - 1
SLOTS = POS * SEQS
SHIFT = 64.0
EPS = 1e-5
BIG = 1e30

f32 = mybir.dt.float32
i32 = mybir.dt.int32
u32 = mybir.dt.uint32
ALU = mybir.AluOpType
ACT = mybir.ActivationFunctionType
AX = mybir.AxisListType


class Order:

    def __init__(self, eng, sem):
        self.eng, self.sem, self.base, self.n = eng, sem, 0, 0

    def link(self, ins):
        ins.then_inc(self.sem, 1)
        self.n += 1
        self.eng.wait_ge(self.sem, self.base + self.n)

    def enter(self, behind):
        self.outer, self.base, self.n = self.base + self.n, self.base + self.n + behind, 0

    def leave(self, turns, per_turn):
        assert self.n == per_turn, f"a turn has {self.n} steps, not {per_turn}"
        self.base, self.n = self.outer + turns * per_turn, 0


def moments(dve, order, stats, mean, spread, veps, sign=1.0):
    even, odd = stats[:, :, 1], stats[:, :, 4]
    dve.tensor_tensor(mean, even, odd, ALU.add)
    dve.tensor_tensor(spread, even, odd, ALU.subtract)
    order.link(dve.tensor_tensor(veps, stats[:, :, 2], stats[:, :, 5], ALU.add))
    dve.tensor_scalar(mean, mean, 0.5 * sign, None, ALU.mult)
    dve.tensor_tensor(spread, spread, spread, ALU.mult)
    order.link(dve.tensor_scalar(veps, veps, 1.0 / D, EPS, ALU.mult, ALU.add))
    return dve.scalar_tensor_tensor(out=veps, in0=spread, scalar=0.25, in1=veps,
                                    op0=ALU.mult, op1=ALU.add)


def build(nc, xT, tok_w, qkv_w, qkv_b, gate_w, gate_b, w1, b1, w2, b2, out):
    ctx = ExitStack()
    with ctx:
        def sb(name, shape, dt=f32, scope=ctx):
            return scope.enter_context(nc.sbuf_tensor(name, shape, dt))

        def pb(name, shape, dt=f32, scope=ctx):
            return scope.enter_context(nc.psum_tensor(name, shape, dt))

        def sem(name):
            return ctx.enter_context(nc.semaphore(name))

        ident = sb("ident", [P, P])
        half_neg = sb("half_neg", [P, SEQS])
        shift_col = sb("shift_col", [P, 1])
        h_all = sb("h_all", [P, POS, SEQS, D])
        qkvw_sb = sb("qkvw_sb", [P, QKV])
        qkvb_sb = sb("qkvb_sb", [P, QKV])
        gatew_sb = sb("gatew_sb", [P, EXPERTS])
        gateb_sb = sb("gateb_sb", [P, EXPERTS])
        w1_sb = sb("w1_sb", [P, EXPERTS, FF])
        w2_sb = sb("w2_sb", [P, EXPERTS, FC, D])
        b1_sb = sb("b1_sb", [P, EXPERTS, FF])
        b2_sb = sb("b2_sb", [P, EXPERTS, D])
        onehot = sb("onehot", [P, POS, SEQS, EXPERTS])
        valid = sb("valid", [P, 1])
        before = sb("before", [P, P])
        ones = sb("ones", [P, P])

        h_dram = nc.dram_tensor("h_rows", (TOK_PAD, D), f32).ap()
        xs_dram = nc.dram_tensor("sorted_rows", (TOK_PAD, D), f32).ap()

        s_w = sem("weights_loaded")
        s_wx = sem("expert_weights_loaded")
        s_init = sem("constants_made")
        s_initg = sem("gpsimd_constants_order")
        s_dve = sem("vector_order")
        s_act = sem("scalar_order")
        s_pool = sem("gpsimd_order")
        s_pad = sem("padding_rows_zeroed")

        rows = ctx.enter_context(ExitStack())
        nT_all = sb("nT_all", [P, SEQS, TP], scope=rows)
        n_aug = sb("n_aug", [P, SEQS, POS, D + 1], scope=rows)

        with ExitStack() as a:
            x_in = [sb(f"x_in{u}", [P, T_IN], scope=a) for u in range(2)]
            tokw_sb = sb("tokw_sb", [P, WINDOW, QKV], scope=a)
            zt = [sb(f"zt{u}", [P, T], scope=a) for u in range(2)]
            ft = [sb(f"ft{u}", [P, T], scope=a) for u in range(2)]
            ot = [sb(f"ot{u}", [P, T], scope=a) for u in range(2)]
            fg = sb("forget", [P, T], scope=a)
            zin = sb("zin", [P, T], scope=a)
            cell = sb("cell", [P, T], scope=a)
            hT = [sb(f"hT{u}", [P, TP], scope=a) for u in range(2)]
            n_st = [sb(f"n_stage{u}", [P, POS, D], scope=a) for u in range(2)]
            stats = sb("stats_a", [P, POS, 6], scope=a)
            mean = sb("mean_a", [P, POS], scope=a)
            spread = sb("spread_a", [P, POS], scope=a)
            veps = sb("var_eps_a", [P, POS], scope=a)
            rstd = sb("rstd_a", [P, POS], scope=a)
            conv = pb("conv", [P, 3, 2, 512], scope=a)
            tr = pb("tr_a", [P, TP], scope=a)

            x_loaded = [sem("x_loaded_even"), sem("x_loaded_odd")]
            s_tokw = sem("conv_weights_loaded")
            conv_done, tanh_done = sem("conv_done"), sem("tanh_done")
            h_ready, hT_done, h_copied = sem("h_ready"), sem("h_transposed"), sem("h_copied")
            var_ready, rstd_ready = sem("var_ready_a"), sem("rstd_ready_a")
            n_ready, nT_done, nT_copied = sem("n_ready"), sem("n_transposed"), sem("nT_copied")
            n_kept = sem("n_kept")

            with nc.Block() as block:
                @block.sync
                def _(sp):
                    sp.dma_start(tokw_sb[:], tok_w).then_inc(s_tokw, 16)
                    for b in range(2):
                        sp.dma_start(x_in[b][:], xT[b]).then_inc(x_loaded[b], 16)
                    for dst, src in ((qkvw_sb, qkv_w), (gatew_sb, gate_w)):
                        sp.dma_start(dst[:], src).then_inc(s_w, 16)
                    sp.dma_start(qkvb_sb[:], qkv_b.partition_broadcast(P)).then_inc(s_w, 16)
                    sp.dma_start(gateb_sb[:], gate_b.partition_broadcast(P)).then_inc(s_w, 16)
                    with sp.Fori(2, SEQS - 1, 2) as b:
                        for u in range(2):
                            sp.wait_ge(conv_done, 3 * (b + u) - 3)
                            sp.dma_start(x_in[u][:], xT[bass.ds(b + u, 1)].rearrange("o p t -> (o p) t")
                                         ).then_inc(x_loaded[u], 16)
                    for dst, src in ((w1_sb, w1), (w2_sb, w2)):
                        sp.dma_start(dst[:], src).then_inc(s_wx, 16)
                    sp.dma_start(b1_sb[:], b1.partition_broadcast(P)).then_inc(s_wx, 16)
                    sp.dma_start(b2_sb[:], b2.partition_broadcast(P)).then_inc(s_wx, 16)

                @block.gpsimd
                def _(pool):
                    order = Order(pool, s_pool)
                    order.link(pool.memset(ident[:], 0.0))
                    pool.affine_select(out=ident[:], in_=ident[:], compare_op=ALU.not_equal, fill=1.0,
                                       base=0, pattern=[[-1, P]], channel_multiplier=1).then_inc(s_init, 1)
                    order.link(pool.memset(ones[:], 1.0))
                    order.link(pool.affine_select(out=before[:], in_=ones[:], compare_op=ALU.is_gt,
                                                  fill=0.0, base=0, pattern=[[1, P]],
                                                  channel_multiplier=-1))
                    order.link(pool.affine_select(out=valid[:], in_=ones[:, 0:1], compare_op=ALU.is_gt,
                                                  fill=0.0, base=T_LAST, pattern=[[0, 1]],
                                                  channel_multiplier=-1))
                    order.link(pool.memset(half_neg[:], -0.5))
                    order.link(pool.memset(shift_col[:], -SHIFT))
                    order.link(pool.memset(n_aug[:, :, :, D], 1.0))
                    for l in range(SEQS):
                        order.link(pool.tensor_copy(n_aug[:, l, POS - 1, D:D + 1], valid[:]))

                    def turn(b, u):
                        pool.wait_ge(var_ready, b + 1)
                        pool.tensor_tensor(rstd[:], veps[:], half_neg[:, 0:POS],
                                           ALU.pow).then_inc(rstd_ready, 1)
                        pool.wait_ge(n_ready, b + 1)
                        pool.tensor_copy(n_aug[:, bass.ds(b, 1), :, 0:D],
                                         n_st[u][:].rearrange("p (o j) d -> p o j d", o=1)
                                         ).then_inc(n_kept, 1)

                    with pool.Fori(0, SEQS - 1, 2) as b:
                        for u in range(2):
                            turn(b + u, u)

                @block.scalar
                def _(act):
                    def tanhs(b, u):
                        if not isinstance(b, int) or b >= 2:
                            act.wait_ge(h_ready, b - 1)
                        for g, (dst, scale) in enumerate(((zt[u], 1.0), (ft[u], 0.5), (ot[u], 0.5))):
                            act.wait_ge(conv_done, 3 * b + g + 1)
                            act.activation(dst[:].rearrange("p (h t) -> p h t", h=2),
                                           conv[:, g, :, 0:HALF], ACT.Tanh,
                                           scale=scale).then_inc(tanh_done, 1)

                    def keep_nT(b):
                        act.wait_ge(nT_done, b + 1)
                        act.activation(nT_all[:, bass.ds(b, 1), :].rearrange("p o t -> p (o t)"),
                                       tr[:], ACT.Copy).then_inc(nT_copied, 1)

                    def keep_h(b):
                        act.wait_ge(n_ready, b + 1)
                        act.activation(h_all[:, :, bass.ds(b, 1), :],
                                       tr[:].rearrange("p (j o d) -> p j o d", o=1, d=D),
                                       ACT.Copy).then_inc(h_copied, 1)

                    tanhs(0, 0)
                    tanhs(1, 1)
                    keep_h(0)
                    with act.Fori(1, SEQS - 2, 2) as b:
                        for u in range(2):
                            tanhs(b + u + 1, u)
                            keep_nT(b + u - 1)
                            keep_h(b + u)
                    keep_nT(SEQS - 2)
                    keep_h(SEQS - 1)
                    keep_nT(SEQS - 1)

                @block.vector
                def _(dve):
                    order = Order(dve, s_dve)
                    for u in range(2):
                        order.link(dve.memset(hT[u][:, T:TP], 0.0))

                    def recur(b, u):
                        dve.wait_ge(tanh_done, 3 * b + 2)
                        dve.tensor_scalar(fg[:], ft[u][:], 0.5, 0.5, ALU.mult, ALU.add)
                        order.link(dve.tensor_scalar(zin[:], ft[u][:], -0.25, 0.25, ALU.mult, ALU.add))
                        order.link(dve.tensor_tensor(zin[:], zin[:], zt[u][:], ALU.mult))
                        order.link(dve.tensor_tensor_scan(cell[:], fg[:], zin[:], 0.0,
                                                          ALU.mult, ALU.add))
                        dve.wait_ge(tanh_done, 3 * b + 3)
                        if not isinstance(b, int) or b >= 2:
                            dve.wait_ge(hT_done, b - 1)
                        dve.scalar_tensor_tensor(out=hT[u][:, 0:T], in0=ot[u][:], scalar=1.0,
                                                 in1=cell[:], op0=ALU.add,
                                                 op1=ALU.mult).then_inc(h_ready, 1)

                    def norm(b, u):
                        dve.wait_ge(hT_done, b + 1)
                        for j in range(POS):
                            last = dve.bn_stats(stats[:, j, :], tr[:, j * D:(j + 1) * D])
                        order.link(last)
                        moments(dve, order, stats, mean[:], spread[:], veps[:]).then_inc(var_ready, 1)
                        dve.wait_ge(rstd_ready, b + 1)
                        if not isinstance(b, int) or b >= 2:
                            dve.wait_ge(nT_done, b - 1)
                            dve.wait_ge(n_kept, b - 1)
                        for j in range(POS):
                            last = dve.tensor_scalar(n_st[u][:, j, :], tr[:, j * D:(j + 1) * D],
                                                     mean[:, j:j + 1], rstd[:, j:j + 1],
                                                     ALU.subtract, ALU.mult)
                        last.then_inc(n_ready, 1)

                    recur(0, 0)
                    recur(1, 1)
                    norm(0, 0)
                    recur(2, 0)
                    norm(1, 1)
                    per = 2 * 6
                    with dve.Fori(2, SEQS - 3, 2) as b:
                        order.enter((b - 2) * (per // 2))
                        for u in range(2):
                            recur(b + u + 1, 1 - u)
                            norm(b + u, u)
                    order.leave((SEQS - 4) // 2, per)
                    recur(SEQS - 1, 1)
                    norm(SEQS - 2, 0)
                    norm(SEQS - 1, 1)

                @block.tensor
                def _(pe):
                    pe.wait_ge(s_tokw, 16)
                    pe.wait_ge(s_init, 1)

                    def convolve(b, u, loaded):
                        pe.wait_ge(x_loaded[u], loaded)
                        for g in range(3):
                            if not isinstance(b, int) or b >= 1:
                                pe.wait_ge(tanh_done, 3 * b + g - 2)
                            for half in range(2):
                                for w in range(WINDOW):
                                    at = half * HALF + w
                                    last = pe.matmul(conv[:, g, half, 0:HALF],
                                                     tokw_sb[:, w, g * D:(g + 1) * D],
                                                     x_in[u][:, at:at + HALF],
                                                     start=(w == 0), stop=(w == WINDOW - 1))
                            last.then_inc(conv_done, 1)

                    def transpose_n(b, u):
                        pe.wait_ge(h_copied, b + 1)
                        for j in range(POS):
                            last = pe.transpose(tr[:, j * P:(j + 1) * P], n_st[u][:, j, :], ident[:])
                        last.then_inc(nT_done, 1)

                    def transpose_h(b, u):
                        pe.wait_ge(h_ready, b + 1)
                        if not isinstance(b, int) or b >= 1:
                            pe.wait_ge(nT_copied, b)
                        for j in range(POS):
                            last = pe.transpose(tr[:, j * P:(j + 1) * P],
                                                hT[u][:, j * P:(j + 1) * P], ident[:])
                        last.then_inc(hT_done, 1)

                    convolve(0, 0, 16)
                    convolve(1, 1, 16)
                    transpose_h(0, 0)
                    with pe.Fori(1, SEQS - 2, 2) as b:
                        for u in range(2):
                            convolve(b + u + 1, u, 8 * b + 24)
                            transpose_n(b + u - 1, u)
                            transpose_h(b + u, 1 - u)
                    transpose_n(SEQS - 2, 0)
                    transpose_h(SEQS - 1, 1)
                    transpose_n(SEQS - 1, 1)

        with ExitStack() as b_:
            expo = [sb(f"expo{u}", [P, POS, P], scope=b_) for u in range(2)]
            pv_sb = sb("pv_sb", [P, SEQS, D + 1], scope=b_)
            rec = sb("rec", [P, SEQS], scope=b_)
            h1 = sb("h1", [P, SEQS, D], scope=b_)
            h2 = sb("h2", [P, SEQS, D], scope=b_)
            nw = sb("n_work", [P, SEQS, D], scope=b_)
            h3 = sb("h3", [P, SEQS, D], scope=b_)
            n3 = sb("n3", [P, SEQS, D], scope=b_)
            nTw = sb("n_work_T", [P, SEQS, P], scope=b_)
            qkv = sb("qkv", [P, SEQS, QKV], scope=b_)
            prod = [sb(f"prod{u}", [P, HEADS, SEQS, HD], scope=b_) for u in range(2)]
            nbias = sb("minus_mean_rstd", [P, SEQS], scope=b_)
            prodp = [sb(f"prod_pool{u}", [P, HEADS, SEQS, HD], scope=b_) for u in range(2)]
            scores = sb("scores", [P, SEQS, HEADS, SEQS], scope=b_)
            notmask = sb("notmask", [P, SEQS, HEADS, SEQS], scope=b_)
            probs = sb("probs", [P, SEQS, HEADS, SEQS], scope=b_)
            top = sb("top", [P, SEQS, HEADS], scope=b_)
            att = sb("att", [P, SEQS, D], scope=b_)
            statsb = sb("stats_b", [P, SEQS, 6], scope=b_)
            meanb = sb("mean_b", [P, SEQS], scope=b_)
            spreadb = sb("spread_b", [P, SEQS], scope=b_)
            vepsb = sb("var_eps_b", [P, SEQS], scope=b_)
            rstdb = sb("rstd_b", [P, SEQS], scope=b_)
            logit = sb("logit", [P, SEQS, EXPERTS], scope=b_)
            elog = sb("exp_logit", [P, SEQS, EXPERTS], scope=b_)
            mxl = sb("max_logit", [P, SEQS], scope=b_)
            best = sb("best", [P, SEQS, EXPERTS], scope=b_)
            firstw = sb("first_weight", [P, EXPERTS], scope=b_)
            s_ps = [pb(f"scores_ps{u}", [P, 1024], scope=b_) for u in range(2)]
            pv_ps = [pb(f"pv_ps{u}", [P, 512], scope=b_) for u in range(2)]
            t_ps = [pb(f"t_ps{u}", [P, 512], scope=b_) for u in range(2)]
            g_ps = pv_ps[0]

            def q_ps(l):
                return s_ps[l // 2 % 2][:, l % 2 * 512:l % 2 * 512 + QKV]

            s_dveb = sem("vector_order_b")
            s_done, exp_done = sem("nn_done"), sem("exp_done")
            pv_done, pv_copied, pv_read = sem("pv_done"), sem("pv_copied"), sem("pv_read")
            varb_ready, rstdb_ready = sem("var_ready_b"), sem("rstd_ready_b")
            n2_ready, n3_ready = sem("n2_ready"), sem("n3_ready")
            t_done, t_copied = sem("t_done"), sem("t_copied")
            q_done, q_read = sem("qkv_done"), sem("qkv_read")
            g_done, g_read = sem("gate_done"), sem("gate_read")
            sm_ready, sm_done = sem("head_scores_ready"), sem("head_exp_done")
            probs_ready, av_ready, av_read = sem("probs_ready"), sem("av_ready"), sem("av_read")
            n1_ready, xs_ready = sem("n1_ready"), sem("expert_rows_ready")
            rec_ready, h1_ready = sem("rec_ready"), sem("h1_ready")
            h2_ready, h2_kept = sem("h2_ready"), sem("h2_kept")
            scp_ready, scp_read = sem("pool_scores_ready"), sem("pool_scores_read")
            s_poolb = sem("gpsimd_order_b")
            h3_ready, h3_stored = sem("h3_ready"), sem("h3_stored")
            lg_ready, lg_done = sem("logits_ready"), sem("logits_exp_done")

            def known(v):
                return isinstance(v, int)

            def at(v):
                return bass.ds(v, 1)

            POOL_L = (1, 3, 5, 7)
            OWN_AV = (0, 4)
            POOL_AV = tuple(l for l in range(SEQS) if l not in OWN_AV)
            ALL = SEQS * POS

            def upto(v, most):
                return min(v, most) if known(v) else v

            def t_before_project(i):
                return 4 * i - 2 if not known(i) or i else 0

            def t_before_gate(i):
                return upto(4 * i + 4, 4 * POS - 2)

            def ln_last(i):
                return upto(3 * i + 2, 3 * POS)

            def ln_first(i):
                return 3 * i + 3

            def schedule(turn, loop):
                turn(0)
                with loop(1, POS - 2) as i:
                    turn(i)
                turn(POS - 2)
                turn(POS - 1)

            def more(i, ahead):
                return not known(i) or i + ahead < POS

            def later(i):
                return not known(i) or i >= 1

            with nc.Block() as block:
                @block.tensor
                def _(pe):
                    def self_attention(i):
                        def nn(l):
                            if not (known(i) and i == 0 and l < 2):
                                pe.wait_ge(exp_done, SEQS * i + l - 1)
                            for j in range(POS):
                                last = pe.matmul(s_ps[l % 2][:, j * P:(j + 1) * P],
                                                 nT_all[:, l, j * P:(j + 1) * P],
                                                 nT_all[:, l, bass.ds(i * P, P)], start=True, stop=True)
                            last.then_inc(s_done, 1)

                        def pv(l):
                            pe.wait_ge(exp_done, SEQS * i + l + 1)
                            if not (known(i) and i == 0 and l < 2):
                                pe.wait_ge(pv_copied, SEQS * i + l - 1)
                            for j in range(POS):
                                last = pe.matmul(pv_ps[l % 2][:, 0:D + 1], expo[l % 2][:, j, :],
                                                 n_aug[:, l, j, :], start=(j == 0), stop=(j == POS - 1))
                            last.then_inc(pv_done, 1)

                        nn(0)
                        for l in range(1, SEQS):
                            nn(l)
                            pv(l - 1)
                        pv(SEQS - 1)

                    def transpose_4(src, group, t_before):
                        if not known(t_before) or t_before + group > 1:
                            pe.wait_ge(t_copied, t_before + group - 1)
                        for m in range(4):
                            last = pe.transpose(t_ps[group][:, m * P:(m + 1) * P],
                                                src[:, 4 * group + m, :], ident[:])
                        last.then_inc(t_done, 1)

                    def gate(i):
                        pe.wait_ge(n3_ready, i + 1)
                        for group in range(2):
                            transpose_4(n3, group, t_before_gate(i))
                        pe.wait_ge(t_copied, t_before_gate(i) + 2)
                        pe.wait_ge(pv_copied, upto(SEQS * (i + 4), ALL))
                        for l in range(SEQS):
                            last = pe.matmul(g_ps[:, l * EXPERTS:(l + 1) * EXPERTS], nTw[:, l, :],
                                             gatew_sb[:], start=True, stop=True)
                        last.then_inc(g_done, 1)

                    def project(i):
                        pe.wait_ge(n2_ready, i + 1)
                        for group in range(2):
                            transpose_4(nw, group, t_before_project(i))
                        pe.wait_ge(t_copied, t_before_project(i) + 2)
                        pe.wait_ge(exp_done, upto(SEQS * (i + 2), ALL))
                        if later(i):
                            pe.wait_ge(q_read, SEQS * i)
                        for l in range(SEQS):
                            if l >= 4:
                                pe.wait_ge(q_read, SEQS * i + l - 3)
                            pe.matmul(q_ps(l), nTw[:, l, :], qkvw_sb[:],
                                      start=True, stop=True).then_inc(q_done, 1)

                    def turn(i):
                        if more(i, 2):
                            pe.wait_ge(q_read, SEQS * (i + 1))
                            if later(i):
                                pe.wait_ge(g_read, i)
                            self_attention(i + 2)
                        if later(i):
                            gate(i - 1)
                        if more(i, 1):
                            project(i + 1)

                    self_attention(0)
                    self_attention(1)
                    project(0)
                    schedule(turn, pe.Fori)
                    pe.wait_ge(g_read, POS)
                    gate(POS - 1)

                @block.scalar
                def _(act):
                    def self_attention(i, between=None):
                        for l in range(SEQS + 1):
                            if l < SEQS:
                                act.wait_ge(s_done, SEQS * i + l + 1)
                                if not known(i) or SEQS * i + l >= 2:
                                    act.wait_ge(pv_done, SEQS * i + l - 1)
                                act.activation(expo[l % 2][:].rearrange("p a b -> p (a b)"),
                                               s_ps[l % 2][:, 0:TP], ACT.Exp,
                                               bias=shift_col[:]).then_inc(exp_done, 1)
                            if l == 1 and later(i):
                                act.wait_ge(pv_read, i)
                            if l >= 1:
                                act.wait_ge(pv_done, SEQS * i + l)
                                act.activation(pv_sb[:, l - 1, :], pv_ps[(l - 1) % 2][:, 0:D + 1],
                                               ACT.Copy).then_inc(pv_copied, 1)
                            if between and l in between:
                                between[l]()

                    def copy_t(t_before, group):
                        act.wait_ge(t_done, t_before + group + 1)
                        act.activation(nTw[:, 4 * group:4 * group + 4, :].rearrange("p a b -> p (a b)"),
                                       t_ps[group][:], ACT.Copy).then_inc(t_copied, 1)

                    def apply(src, dst, n, ready):
                        act.wait_ge(rstdb_ready, n)
                        for l in range(SEQS):
                            last = act.activation(dst[:, l, :], src[:, l, :], ACT.Identity,
                                                  bias=nbias[:, l:l + 1], scale=rstdb[:, l:l + 1])
                        last.then_inc(ready, 1)

                    def norm_h1(i):
                        if later(i):
                            act.wait_ge(t_done, t_before_project(i - 1) + 2)
                        apply(h1, nw, ln_first(i - 1) if later(i) else 1, n1_ready)

                    def norm_h2(i):
                        apply(h2, nw, ln_first(i - 1) + 1 if later(i) else 2, n2_ready)

                    def norm_h3(i):
                        act.wait_ge(xs_ready, i + 1)
                        apply(h3, n3, upto(3 * i + 5, 3 * POS), n3_ready)

                    def head_exp(i):
                        act.wait_ge(sm_ready, i + 1)
                        act.activation(probs[:], probs[:], ACT.Exp).then_inc(sm_done, 1)

                    def gate_copies(i):
                        act.wait_ge(q_done, upto(SEQS * (i + 2), ALL))
                        for group in range(2):
                            copy_t(t_before_gate(i), group)

                    def project_copies(i):
                        for group in range(2):
                            copy_t(t_before_project(i), group)

                    def gate_exp(i):
                        act.wait_ge(lg_ready, i + 1)
                        act.activation(elog[:], logit[:], ACT.Exp).then_inc(lg_done, 1)

                    def keep_h2(i):
                        act.wait_ge(h2_ready, i + 1)
                        act.activation(h_all[:, at(i)].rearrange("p o l d -> p (o l) d"), h2[:],
                                       ACT.Copy).then_inc(h2_kept, 1)

                    def turn(i):
                        woven = {5: lambda: head_exp(i)}
                        if later(i):
                            woven[1] = lambda: norm_h3(i - 1)
                        if more(i, 1):
                            woven[3] = lambda: norm_h1(i + 1)
                        if more(i, 2):
                            self_attention(i + 2, woven)
                        else:
                            for l in sorted(woven):
                                woven[l]()
                        if later(i):
                            gate_copies(i - 1)
                        if more(i, 1):
                            norm_h2(i + 1)
                            keep_h2(i + 1)
                            project_copies(i + 1)
                        if later(i):
                            gate_exp(i - 1)

                    self_attention(0)
                    self_attention(1, {2: lambda: norm_h1(0), 4: lambda: norm_h2(0)})
                    keep_h2(0)
                    project_copies(0)
                    schedule(turn, act.Fori)
                    norm_h3(POS - 1)
                    gate_copies(POS - 1)
                    gate_exp(POS - 1)

                @block.gpsimd
                def _(pool):
                    order = Order(pool, s_poolb)
                    heads = qkv[:].rearrange("p m (h c) -> p h m c", c=3 * HD)
                    key_rows, value_rows = heads[:, :, :, HD:2 * HD], heads[:, :, :, 2 * HD:]

                    def rstd_of(n, used=None, times=0):
                        if used:
                            pool.wait_ge(used, times)
                        pool.wait_ge(varb_ready, n)
                        order.link(pool.tensor_tensor(rstdb[:], vepsb[:], half_neg[:], ALU.pow))
                        pool.tensor_tensor(nbias[:], meanb[:], rstdb[:], ALU.mult
                                           ).then_inc(rstdb_ready, 1)

                    def unnormed(i):
                        pool.wait_ge(rec_ready, i + 1)
                        if later(i):
                            pool.wait_ge(h2_ready, i)
                        pool.tensor_tensor(h1[:], pv_sb[:, :, 0:D],
                                           rec[:].unsqueeze(2).broadcast_to([P, SEQS, D]),
                                           ALU.mult).then_inc(pv_read, 1)

                    def residual(i):
                        pool.wait_ge(pv_read, i + 1)
                        order.link(pool.tensor_tensor(h1[:], h1[:], n_aug[:, :, at(i), 0:D].rearrange(
                            "p l o d -> p (l o) d"), ALU.mult))
                        pool.tensor_tensor(h1[:], h1[:], h_all[:, at(i)].rearrange(
                            "p o l d -> p (o l) d"), ALU.add).then_inc(h1_ready, 1)

                    def score_product(i, n):
                        reads = len(POOL_L) * i + n - 2
                        if not known(reads) or reads >= 0:
                            pool.wait_ge(scp_read, reads + 1)
                        query = heads[:, :, POOL_L[n], 0:HD].unsqueeze(2).broadcast_to(
                            [P, HEADS, SEQS, HD])
                        pool.tensor_tensor(prodp[n % 2][:], query, key_rows, ALU.mult
                                           ).then_inc(scp_ready, 1)

                    def turn(i):
                        if more(i, 1):
                            unnormed(i + 1)
                            residual(i + 1)
                        pool.wait_ge(q_read, SEQS * (i + 1))
                        for n in range(len(POOL_L)):
                            score_product(i, n)
                            if n == 0 and later(i):
                                rstd_of(ln_last(i), n2_ready, i + 1)
                            if n == 1 and more(i, 1):
                                if later(i):
                                    rstd_of(ln_first(i), n3_ready, i)
                                else:
                                    rstd_of(ln_first(i), n2_ready, 1)
                        if more(i, 1):
                            rstd_of(ln_first(i) + 1, n1_ready, i + 2)
                        pool.wait_ge(probs_ready, i + 1)
                        for n, l in enumerate(POOL_AV):
                            if n >= 2:
                                pool.wait_ge(av_read, SEQS * i + POOL_AV[n - 2] + 1)
                            pool.tensor_tensor(
                                prod[n % 2][:],
                                probs[:, l, :, :].unsqueeze(3).broadcast_to([P, HEADS, SEQS, HD]),
                                value_rows, ALU.mult).then_inc(av_ready, 1)

                    unnormed(0)
                    residual(0)
                    rstd_of(1)
                    rstd_of(2, n1_ready, 1)
                    turn(0)
                    with pool.Fori(1, POS - 2) as i:
                        order.enter((i - 1) * 4)
                        turn(i)
                    order.leave(POS - 3, 4)
                    turn(POS - 2)
                    turn(POS - 1)
                    rstd_of(3 * POS, n3_ready, POS - 1)

                @block.sync
                def _(sp):
                    rows_of = h_dram[0:TOKENS].rearrange("(l t) d -> t l d", l=SEQS)
                    with sp.Fori(0, POS - 1) as i:
                        sp.wait_ge(h3_ready, i + 1)
                        sp.dma_start(rows_of[bass.ds(i * P, P)], h3[:]).then_inc(h3_stored, 16)
                    sp.wait_ge(h3_ready, POS)
                    sp.dma_start(rows_of[(POS - 1) * P:T], h3[0:T_LAST]).then_inc(h3_stored, 16)

                @block.vector
                def _(dve):
                    order = Order(dve, s_dveb)
                    for e in range(EXPERTS):
                        last = dve.memset(firstw[:, e:e + 1], float(EXPERTS - e))
                    order.link(last)
                    dve.wait_ge(s_w, 64)

                    def wide(col, n):
                        return col.unsqueeze(2).broadcast_to([P, SEQS, n])

                    def row_stats(src, n):
                        for l in range(SEQS):
                            last = dve.bn_stats(statsb[:, l, :], src[:, l, :])
                        order.link(last)
                        row_moments(n)

                    def row_moments(n):
                        if not known(n) or n >= 2:
                            dve.wait_ge(rstdb_ready, n - 1)
                        moments(dve, order, statsb, meanb[:], spreadb[:], vepsb[:], sign=-1.0
                                ).then_inc(varb_ready, 1)

                    def sums(i):
                        dve.wait_ge(pv_copied, SEQS * (i + 1))
                        dve.reciprocal(rec[:], pv_sb[:, :, D]).then_inc(rec_ready, 1)

                    def stats_h1(i, n):
                        dve.wait_ge(h1_ready, i + 1)
                        row_stats(h1, n)

                    def second_residual(i, n):
                        if later(i):
                            dve.wait_ge(h2_kept, i)
                        dve.wait_ge(n1_ready, i + 1)
                        dve.tensor_tensor(h2[:], h1[:], nw[:], ALU.add).then_inc(h2_ready, 1)
                        dve.wait_ge(h2_ready, i + 1)
                        row_stats(h2, n)

                    def head_scores(i):
                        if more(i, 1):
                            sums(i + 1)
                        for l in range(SEQS):
                            dve.wait_ge(q_done, SEQS * i + l + 1)
                            dve.tensor_tensor(qkv[:, l, :], q_ps(l), qkvb_sb[:],
                                              ALU.add).then_inc(q_read, 1)
                            if later(i):
                                last = dve.bn_stats(statsb[:, l, :], h3[:, l, :])
                        if later(i):
                            order.link(last)
                            row_moments(ln_last(i))
                        dve.wait_ge(q_read, SEQS * (i + 1))
                        heads = qkv[:].rearrange("p m (h c) -> p h m c", c=3 * HD)
                        for l in range(SEQS):
                            if l in POOL_L:
                                n = POOL_L.index(l)
                                dve.wait_ge(scp_ready, len(POOL_L) * i + n + 1)
                                dve.tensor_reduce(scores[:, l], prodp[n % 2][:], AX.X, ALU.add
                                                  ).then_inc(scp_read, 1)
                            else:
                                query = heads[:, :, l, 0:HD].unsqueeze(2).broadcast_to(
                                    [P, HEADS, SEQS, HD])
                                own = l // 2 % 2
                                order.link(dve.tensor_tensor(prod[own][:], query,
                                                             heads[:, :, :, HD:2 * HD], ALU.mult))
                                order.link(dve.tensor_reduce(scores[:, l], prod[own][:], AX.X, ALU.add))
                            if l == 1 and more(i, 1):
                                stats_h1(i + 1, ln_first(i))
                            if l == 6 and more(i, 1):
                                second_residual(i + 1, ln_first(i) + 1)
                        dve.wait_ge(scp_read, len(POOL_L) * (i + 1))

                    def head_softmax(i):
                        flat = "p l h m -> p (l h) m"
                        sc, nm, pr = (x[:].rearrange(flat) for x in (scores, notmask, probs))
                        tp = top[:].rearrange("p l h -> p (l h)")
                        tpw = tp.unsqueeze(2).broadcast_to([P, SEQS * HEADS, SEQS])
                        order.link(dve.tensor_scalar(nm, sc, HD ** -0.5, 0.0, ALU.mult, ALU.not_equal))
                        order.link(dve.tensor_scalar(pr, nm, BIG, -BIG, ALU.mult, ALU.add))
                        order.link(dve.scalar_tensor_tensor(out=pr, in0=sc, scalar=HD ** -0.5, in1=pr,
                                                            op0=ALU.mult, op1=ALU.add))
                        order.link(dve.tensor_reduce(tp, pr, AX.X, ALU.max))
                        dve.tensor_tensor(pr, pr, tpw, ALU.subtract).then_inc(sm_ready, 1)
                        dve.wait_ge(sm_done, i + 1)
                        order.link(dve.tensor_tensor(pr, pr, nm, ALU.mult))
                        order.link(dve.tensor_reduce(tp, pr, AX.X, ALU.add))
                        order.link(dve.tensor_scalar(tp, tp, 1.0 / BIG, None, ALU.max))
                        order.link(dve.reciprocal(tp, tp))
                        dve.tensor_tensor(pr, pr, tpw, ALU.mult).then_inc(probs_ready, 1)

                    def head_values(i):
                        heads = qkv[:].rearrange("p m (h c) -> p h m c", c=3 * HD)
                        for l in range(SEQS):
                            if l in OWN_AV:
                                dve.wait_ge(probs_ready, i + 1)
                                weight = probs[:, l, :, :].unsqueeze(3).broadcast_to(
                                    [P, HEADS, SEQS, HD])
                                product = prodp[OWN_AV.index(l) % 2]
                                order.link(dve.tensor_tensor(product[:], weight,
                                                             heads[:, :, :, 2 * HD:], ALU.mult))
                            else:
                                n = POOL_AV.index(l)
                                product = prod[n % 2]
                                dve.wait_ge(av_ready, len(POOL_AV) * i + n + 1)
                            dve.tensor_reduce(att[:, l, :].rearrange("p (h c) -> p h c", c=HD),
                                              product[:].rearrange("p h m c -> p h c m"),
                                              AX.X, ALU.add).then_inc(av_read, 1)
                        dve.wait_ge(av_read, SEQS * (i + 1))
                        if later(i):
                            dve.wait_ge(h3_stored, 16 * i)
                            dve.wait_ge(n3_ready, i)
                        dve.wait_ge(h2_kept, i + 1)
                        dve.tensor_tensor(h3[:], h_all[:, at(i)].rearrange("p o l d -> p (o l) d"),
                                          att[:], ALU.add).then_inc(h3_ready, 1)
                        dve.wait_ge(h3_ready, i + 1)

                    def route(i):
                        dve.wait_ge(g_done, i + 1)
                        dve.tensor_tensor(
                            logit[:], g_ps[:, 0:SEQS * EXPERTS].rearrange("p (l e) -> p l e", e=EXPERTS),
                            gateb_sb[:].unsqueeze(1).broadcast_to([P, SEQS, EXPERTS]),
                            ALU.add).then_inc(g_read, 1)
                        dve.wait_ge(g_read, i + 2)
                        oh = onehot[:, at(i)].rearrange("p o l e -> p (o l) e")
                        order.link(dve.tensor_reduce(mxl[:], logit[:], AX.X, ALU.max))
                        order.link(dve.tensor_tensor(best[:], logit[:], wide(mxl[:], EXPERTS),
                                                     ALU.is_equal))
                        dve.tensor_tensor(logit[:], logit[:], wide(mxl[:], EXPERTS),
                                          ALU.subtract).then_inc(lg_ready, 1)
                        order.link(dve.tensor_tensor(
                            best[:], best[:], firstw[:].unsqueeze(1).broadcast_to([P, SEQS, EXPERTS]),
                            ALU.mult))
                        order.link(dve.tensor_reduce(mxl[:], best[:], AX.X, ALU.max))
                        order.link(dve.tensor_tensor(oh, best[:], wide(mxl[:], EXPERTS), ALU.is_equal))
                        if known(i) and i == POS - 1:
                            dve.tensor_scalar(oh, oh, valid[:], None, ALU.mult)
                        dve.wait_ge(lg_done, i + 1)
                        order.link(dve.tensor_reduce(mxl[:], elog[:], AX.X, ALU.add))
                        order.link(dve.reciprocal(mxl[:], mxl[:]))
                        dve.tensor_tensor(h_all[:, at(i)].rearrange("p o l d -> p (o l) d"),
                                          n3[:], wide(mxl[:], D), ALU.mult).then_inc(xs_ready, 1)

                    def turn(i):
                        head_scores(i)
                        head_softmax(i)
                        head_values(i)
                        if later(i):
                            route(i - 1)

                    dve.memset(logit[:], 0.0).then_inc(g_read, 1)
                    dve.memset(best[:], 0.0).then_inc(xs_ready, 1)
                    sums(0)
                    stats_h1(0, 1)
                    second_residual(0, 2)
                    turn(0)
                    per = 34
                    with dve.Fori(1, POS - 2) as i:
                        order.enter((i - 1) * per)
                        turn(i)
                    order.leave(POS - 3, per)
                    turn(POS - 2)
                    turn(POS - 1)
                    row_stats(h3, 3 * POS)
                    route(POS - 1)
        rows.close()
        place = sb("place", [P, POS, SEQS], u32)
        tile_of = sb("tile_of", [P, PAIRS], i32)
        expert_of = sb("expert_of", [P, PAIRS], i32)
        owned = sb("owned", [P, PAIRS])
        with ExitStack() as c_:
            total = sb("total", [P, EXPERTS, SEQS, POS], scope=c_)
            upto = sb("upto", [P, EXPERTS, SEQS, POS], scope=c_)
            below = sb("below", [P, EXPERTS, SEQS, POS], scope=c_)
            ones_row = sb("ones_row", [P, EXPERTS * SLOTS], scope=c_)
            spot = sb("spot", [P, POS, SEQS, EXPERTS], scope=c_)
            placef = sb("placef", [P, SLOTS], scope=c_)
            ints = sb("ints", [P, PAIRS + TILES + EXPERTS + 1], i32, scope=c_)
            nums = sb("nums", [P, PAIRS + TILES + EXPERTS + 1], scope=c_)
            q_row = nums[:, 0:PAIRS]
            cut_row = nums[:, PAIRS + 1:PAIRS + TILES]
            e_row = nums[:, PAIRS + TILES:PAIRS + TILES + EXPERTS]
            p_col = nums[:, PAIRS + TILES + EXPERTS:]
            ends = sb("ends", [P, 4, EXPERTS], scope=c_)
            start, stop, jump, last_tile = (ends[:, n, :] for n in range(4))
            count = sb("pair_count", [P, EXPERTS], scope=c_)
            cincl = sb("pairs_upto", [P, EXPERTS], scope=c_)
            cuts = sb("cuts", [P, EXPERTS, TILES - 1], scope=c_)
            sel = sb("sel", [P, PAIRS, EXPERTS], scope=c_)
            tmp = sb("sel_times", [P, PAIRS, EXPERTS], scope=c_)
            expf = sb("expert_f", [P, PAIRS], scope=c_)
            tilef = sb("tile_f", [P, PAIRS], scope=c_)
            first_row = sb("first_row", [P, PAIRS], scope=c_)
            stop_row = sb("stop_row", [P, PAIRS], scope=c_)
            row = sb("row", [P, PAIRS], scope=c_)
            zeros = sb("zeros", [TOK_PAD - TOKENS, D], scope=c_)
            before_ps = pb("before_ps", [P, 512], scope=c_)
            total_ps = pb("total_ps", [P, 512], scope=c_)
            s_cnt, s_rows, s_place = sem("counted"), sem("index_rows_made"), sem("places_ready")
            s_scat, s_dvec = sem("rows_scattered"), sem("vector_order_c")
            s_zero = sem("zeros_made")

            with nc.Block() as block:
                @block.tensor
                def _(pe):
                    flat = onehot[:].rearrange("p i l e -> p (i l e)")
                    pe.matmul(before_ps[:, 0:SLOTS * EXPERTS], before[:], flat, start=True, stop=True)
                    pe.matmul(total_ps[:, 0:SLOTS * EXPERTS], ones[:], flat,
                              start=True, stop=True).then_inc(s_cnt, 1)

                @block.gpsimd
                def _(pool):
                    pool.memset(zeros[:], 0.0).then_inc(s_zero, 1)
                    for at0, n, step, chan in ((0, PAIRS, 1, 0), (PAIRS, TILES, P, 0),
                                               (PAIRS + TILES, EXPERTS, 1, 0),
                                               (PAIRS + TILES + EXPERTS, 1, 0, 1)):
                        pool.iota(ints[:, at0:at0 + n], pattern=[[step, n]], base=0,
                                  channel_multiplier=chan).then_inc(s_rows, 1)
                    pool.wait_ge(s_place, 1)
                    for i in range(POS):
                        for l in range(SEQS):
                            n = T_LAST if i == POS - 1 else P
                            pool.indirect_dma_start(
                                xs_dram[0:TOKENS, :],
                                bass.IndirectOffsetOnAxis(ap=place[0:n, i, l:l + 1], axis=0),
                                h_all[0:n, i, l, :], None,
                                bounds_check=TOKENS - 1, oob_is_err=False).then_inc(s_scat, 16)
                    pool.wait_ge(s_scat, 16 * SLOTS)

                @block.sync
                def _(sp):
                    sp.wait_ge(s_zero, 1)
                    for dst in (xs_dram, h_dram):
                        sp.dma_start(dst[TOKENS:TOK_PAD], zeros[:]).then_inc(s_pad, 16)
                    sp.wait_ge(s_pad, 32)

                @block.vector
                def _(dve):
                    order = Order(dve, s_dvec)
                    order.link(dve.memset(ones_row[:], 1.0))
                    dve.wait_ge(s_cnt, 1)
                    order.link(dve.tensor_copy(total[:], total_ps[:, 0:SLOTS * EXPERTS].rearrange(
                        "p (i l e) -> p e l i", i=POS, l=SEQS)))
                    run = "p e l i -> p (e l i)"
                    order.link(dve.tensor_tensor_scan(upto[:].rearrange(run), ones_row[:],
                                                      total[:].rearrange(run), 0.0, ALU.mult, ALU.add))
                    order.link(dve.tensor_tensor(below[:].rearrange(run), upto[:].rearrange(run),
                                                 total[:].rearrange(run), ALU.subtract))
                    for e in range(EXPERTS):
                        last = dve.tensor_tensor(
                            spot[:, :, :, e],
                            before_ps[:, 0:SLOTS * EXPERTS].rearrange("p (i l e) -> p i l e", i=POS,
                                                                      l=SEQS)[:, :, :, e],
                            below[:, e].rearrange("p l i -> p i l"), ALU.add)
                    order.link(last)
                    order.link(dve.tensor_tensor(spot[:], spot[:], onehot[:], ALU.mult))
                    order.link(dve.tensor_reduce(placef[:], spot[:].rearrange("p i l e -> p (i l) e"),
                                                 AX.X, ALU.add))
                    dve.tensor_copy(place[:].rearrange("p i l -> p (i l)"),
                                    placef[:]).then_inc(s_place, 1)

                    dve.wait_ge(s_rows, 4)
                    dve.tensor_copy(nums[:], ints[:])
                    dve.tensor_copy(start, below[:, :, 0, 0])
                    order.link(dve.tensor_copy(stop, upto[:, :, SEQS - 1, POS - 1]))

                    def tiles_before(dst, bound, compare):
                        cut = cut_row.unsqueeze(1).broadcast_to([P, EXPERTS, TILES - 1])
                        order.link(dve.tensor_tensor(
                            cuts[:], bound.unsqueeze(2).broadcast_to([P, EXPERTS, TILES - 1]), cut,
                            compare))
                        order.link(dve.tensor_reduce(dst, cuts[:], AX.X, ALU.add))

                    tiles_before(jump, start, ALU.is_ge)
                    tiles_before(last_tile, stop, ALU.is_gt)
                    order.link(dve.tensor_tensor(count[:], last_tile, jump, ALU.subtract))
                    dve.tensor_tensor(last_tile, stop, start, ALU.is_gt)
                    order.link(dve.tensor_scalar(count[:], count[:], 1.0, None, ALU.add))
                    order.link(dve.tensor_tensor(count[:], count[:], last_tile, ALU.mult))
                    order.link(dve.tensor_tensor_scan(cincl[:], ones_row[:, 0:EXPERTS], count[:], 0.0,
                                                      ALU.mult, ALU.add))
                    order.link(dve.tensor_tensor(count[:], cincl[:], count[:], ALU.subtract))
                    order.link(dve.tensor_tensor(jump, jump, count[:], ALU.subtract))

                    def by_pair(v):
                        return v.unsqueeze(2).broadcast_to([P, PAIRS, EXPERTS])

                    def by_expert(v):
                        return v.unsqueeze(1).broadcast_to([P, PAIRS, EXPERTS])

                    order.link(dve.tensor_tensor(tmp[:], by_pair(q_row), by_expert(cincl[:]), ALU.is_ge))
                    order.link(dve.tensor_reduce(expf[:], tmp[:], AX.X, ALU.add))
                    order.link(dve.tensor_scalar(expf[:], expf[:], EXPERTS - 1.0, None, ALU.min))
                    order.link(dve.tensor_tensor(sel[:], by_pair(expf[:]), by_expert(e_row),
                                                 ALU.is_equal))
                    dve.tensor_copy(expert_of[:], expf[:])
                    for dst, src in ((tilef, jump), (first_row, start), (stop_row, stop)):
                        order.link(dve.tensor_tensor(tmp[:], sel[:], by_expert(src), ALU.mult))
                        order.link(dve.tensor_reduce(dst[:], tmp[:], AX.X, ALU.add))
                    order.link(dve.tensor_tensor(tilef[:], tilef[:], q_row, ALU.add))
                    order.link(dve.tensor_scalar(tilef[:], tilef[:], TILES - 1.0, None, ALU.min))
                    dve.tensor_copy(tile_of[:], tilef[:])
                    order.link(dve.tensor_scalar(row[:], tilef[:], float(P), p_col, ALU.mult, ALU.add))
                    dve.tensor_tensor(first_row[:], row[:], first_row[:], ALU.is_ge)
                    order.link(dve.tensor_tensor(stop_row[:], row[:], stop_row[:], ALU.is_lt))
                    order.link(dve.tensor_tensor(first_row[:], first_row[:], stop_row[:], ALU.mult))
                    order.link(dve.tensor_scalar(row[:], q_row, cincl[:, EXPERTS - 1:], None, ALU.is_lt))
                    order.link(dve.tensor_tensor(owned[:], first_row[:], row[:], ALU.mult))

        with ExitStack() as d_:
            AHEAD = 4
            y = sb("y", [P, TILES, D], scope=d_)
            x_rows = [sb(f"x_rows{u}", [P, D], scope=d_) for u in range(AHEAD)]
            xTd = [sb(f"xT_sorted{u}", [P, P], scope=d_) for u in range(2)]
            hid = [sb(f"hidden{u}", [P, FF], scope=d_) for u in range(2)]
            hidT = [sb(f"hidden_T{u}", [P, FC, P], scope=d_) for u in range(2)]
            yb = sb("y_bias", [P, D], scope=d_)
            x_ps = pb("x_ps", [P, 512], scope=d_)
            hid_ps = [pb(f"hid_ps{u}", [P, FF], scope=d_) for u in range(2)]
            hT_ps = [pb(f"hT_ps{u}", [P, 512], scope=d_) for u in range(2)]
            y_ps = [pb(f"y_ps{u}", [P, 512], scope=d_) for u in range(2)]
            y_loaded, s_out = sem("h_rows_loaded"), sem("out_stored")
            rows_in = [sem(f"rows_in{u}") for u in range(AHEAD)]
            x_done, xT_ready = sem("x_transposed"), sem("xT_ready")
            up_done, hid_ready = sem("up_done"), sem("hidden_ready")
            hT_done2, hidT_ready = sem("hidden_transposed"), sem("hidden_T_ready")
            down_done, y_read, y_added = sem("down_done"), sem("y_read"), sem("y_added")
            LAG = EXPERTS
            END = PAIRS + 3

            def steps(step, loop, end, first=2 * AHEAD):
                stop = first + (PAIRS - first) // AHEAD * AHEAD
                for t in range(first):
                    step(t, t % AHEAD)
                with loop(first, stop - AHEAD + 1, AHEAD) as t:
                    for u in range(AHEAD):
                        step(t + u, u)
                for t in range(stop, end):
                    step(t, t % AHEAD)

            def is_int(v):
                return isinstance(v, int)

            with nc.Block() as block:
                @block.sync
                def _(sp):
                    h_tiles = h_dram.rearrange("(k p) d -> p k d", p=P)
                    x_tiles = xs_dram.rearrange("(k p) d -> k p d", p=P)

                    def load(t, u):
                        k = sp.value_load(tile_of[0:1, bass.ds(t, 1)], min_val=0, max_val=TILES - 1)
                        if not is_int(t) or t >= AHEAD:
                            sp.wait_ge(x_done, t - AHEAD + 1)
                        sp.dma_start(x_rows[u][:], x_tiles[bass.ds(k, 1)].rearrange("o p d -> (o p) d")
                                     ).then_inc(rows_in[u], 16)
                        if is_int(t) and t == AHEAD - 1:
                            sp.wait_ge(h3_stored, 16 * POS)
                            sp.dma_start(y[:], h_tiles).then_inc(y_loaded, 16)

                    steps(load, sp.Fori, PAIRS)

                @block.gpsimd
                def _(pool):
                    out_tiles = out[0:(TILES - 1) * P].rearrange("(k p) d -> p k d", p=P)
                    with pool.Fori(LAG, PAIRS) as q:
                        pool.wait_ge(y_added, q + 1)
                        pool.dma_start(out_tiles[:, bass.ds(q - LAG, 1), :],
                                       y[:, bass.ds(q - LAG, 1), :]).then_inc(s_out, 16)
                    pool.dma_start(out[(TILES - 1) * P:TOKENS], y[0:TAIL, TILES - 1, :]).then_inc(s_out, 16)
                    pool.wait_ge(s_out, 16 * TILES)

                @block.tensor
                def _(pe):
                    def step(t, u):
                        r, u, v = u, u % 2, 1 - u % 2
                        if not is_int(t) or t < PAIRS:
                            pe.wait_ge(rows_in[r], 16 // AHEAD * (t - r) + 16)
                            if not is_int(t) or t >= 1:
                                pe.wait_ge(xT_ready, t)
                            pe.transpose(x_ps[:, 0:P], x_rows[r][:], ident[:]).then_inc(x_done, 1)
                        if not is_int(t) or 1 <= t <= PAIRS:
                            e = pe.value_load(expert_of[0:1, bass.ds(t - 1, 1)], min_val=0,
                                              max_val=EXPERTS - 1)
                            pe.wait_ge(xT_ready, t)
                            if not is_int(t) or t >= 3:
                                pe.wait_ge(hid_ready, t - 2)
                            pe.matmul(hid_ps[v][:], xTd[v][:],
                                      w1_sb[:, bass.ds(e, 1), :].rearrange("p o f -> p (o f)"),
                                      start=True, stop=True).then_inc(up_done, 1)
                        if not is_int(t) or 2 <= t <= PAIRS + 1:
                            pe.wait_ge(hid_ready, t - 1)
                            if not is_int(t) or t >= 4:
                                pe.wait_ge(hidT_ready, t - 3)
                            for c in range(FC):
                                last = pe.transpose(hT_ps[u][:, c * P:(c + 1) * P],
                                                    hid[u][:, c * P:(c + 1) * P], ident[:])
                            last.then_inc(hT_done2, 1)
                        if not is_int(t) or t >= 3:
                            e = pe.value_load(expert_of[0:1, bass.ds(t - 3, 1)], min_val=0,
                                              max_val=EXPERTS - 1)
                            pe.wait_ge(hidT_ready, t - 2)
                            if not is_int(t) or t >= 5:
                                pe.wait_ge(y_read, t - 4)
                            for c in range(FC):
                                last = pe.matmul(y_ps[v][:, 0:D], hidT[v][:, c, :],
                                                 w2_sb[:, bass.ds(e, 1), c, :].rearrange(
                                                     "p o d -> p (o d)"),
                                                 start=(c == 0), stop=(c == FC - 1))
                            last.then_inc(down_done, 1)

                    pe.wait_ge(s_wx, 64)
                    steps(step, pe.Fori, END)

                @block.scalar
                def _(act):
                    def step(t, u):
                        u %= 2
                        if not is_int(t) or t < PAIRS:
                            act.wait_ge(x_done, t + 1)
                            if not is_int(t) or t >= 2:
                                act.wait_ge(up_done, t - 1)
                            act.activation(xTd[u][:], x_ps[:, 0:P], ACT.Copy).then_inc(xT_ready, 1)
                        if not is_int(t) or 2 <= t <= PAIRS + 1:
                            act.wait_ge(hT_done2, t - 1)
                            if not is_int(t) or t >= 4:
                                act.wait_ge(down_done, t - 3)
                            act.activation(hidT[u][:].rearrange("p c t -> p (c t)"), hT_ps[u][:],
                                           ACT.Relu).then_inc(hidT_ready, 1)

                    steps(step, act.Fori, END)

                @block.vector
                def _(dve):
                    def step(t, u):
                        u, v = u % 2, 1 - u % 2
                        if not is_int(t) or 1 <= t <= PAIRS:
                            e = dve.value_load(expert_of[0:1, bass.ds(t - 1, 1)], min_val=0,
                                               max_val=EXPERTS - 1)
                            dve.wait_ge(up_done, t)
                            if not is_int(t) or t >= 3:
                                dve.wait_ge(hT_done2, t - 2)
                            dve.tensor_tensor(hid[v][:], hid_ps[v][:],
                                              b1_sb[:, bass.ds(e, 1), :].rearrange("p o f -> p (o f)"),
                                              ALU.add).then_inc(hid_ready, 1)
                        if not is_int(t) or t >= 3:
                            e = dve.value_load(expert_of[0:1, bass.ds(t - 3, 1)], min_val=0,
                                               max_val=EXPERTS - 1)
                            k = dve.value_load(tile_of[0:1, bass.ds(t - 3, 1)], min_val=0,
                                               max_val=TILES - 1)
                            dve.wait_ge(down_done, t - 2)
                            if not is_int(t) or t >= 4:
                                dve.wait_ge(y_added, t - 3)
                            dve.tensor_tensor(yb[:], y_ps[v][:, 0:D],
                                              b2_sb[:, bass.ds(e, 1), :].rearrange("p o d -> p (o d)"),
                                              ALU.add).then_inc(y_read, 1)
                            dve.wait_ge(y_read, t - 2)
                            y_tile = y[:, bass.ds(k, 1), :].rearrange("p o d -> p (o d)")
                            dve.scalar_tensor_tensor(out=y_tile, in0=yb[:],
                                                     scalar=owned[:, bass.ds(t - 3, 1)], in1=y_tile,
                                                     op0=ALU.mult, op1=ALU.add).then_inc(y_added, 1)

                    dve.wait_ge(s_wx, 64)
                    dve.wait_ge(y_loaded, 16)
                    steps(step, dve.Fori, END)


def kernel(x, L0_tok_kernel, L0_ffn_Wa, L0_ffn_ba, L0_ffn_Ws, L0_ffn_bs, L1_attn_W, L1_attn_b,
           L1_ffn_Wg, L1_ffn_bg, L1_ffn_W1, L1_ffn_b1, L1_ffn_W2, L1_ffn_b2):
    import numpy as _np
    import concourse.bacc as _bacc
    from concourse import mybir as _mybir
    from concourse.bass_utils import run_bass_kernel_spmd as _run

    nc = _bacc.Bacc("TRN2", target_bir_lowering=False, num_devices=1)
    laid_out = {
        "xT": _np.asarray(x).transpose(0, 2, 1),
        "tok_w": _np.asarray(L0_tok_kernel).transpose(1, 0, 2),
        "qkv_w": _np.asarray(L1_attn_W).T,
        "qkv_b": _np.asarray(L1_attn_b),
        "gate_w": _np.asarray(L1_ffn_Wg),
        "gate_b": _np.asarray(L1_ffn_bg),
        "w1": _np.asarray(L1_ffn_W1).transpose(1, 0, 2),
        "b1": _np.asarray(L1_ffn_b1),
        "w2": _np.asarray(L1_ffn_W2).reshape(EXPERTS, FC, P, D).transpose(2, 0, 1, 3),
        "b2": _np.asarray(L1_ffn_b2),
    }
    arrays, args = {}, []
    for name, a in laid_out.items():
        a = _np.ascontiguousarray(a)
        arrays[name] = a
        args.append(nc.dram_tensor(name, a.shape, _mybir.dt.from_np(a.dtype), kind="ExternalInput").ap())
    args.append(nc.dram_tensor("out", (TOKENS, D), _mybir.dt.float32, kind="ExternalOutput").ap())
    build(nc, *args)
    r = _run(nc, [arrays], core_ids=[0])
    return r.results[0]["out"].reshape(SEQS, T, D)
```

```python
from contextlib import ExitStack

import concourse.bass as bass
from concourse import mybir

P = 128
SEQS, T_IN, D = 8, 750, 128
WINDOW = 3
T = T_IN - WINDOW + 1
HALF = T // 2
POS = -(-T // P)
TP = POS * P
T_LAST = T - (POS - 1) * P
HEADS, HD = 8, 16
QKV = 3 * D
EXPERTS, FF = 8, 512
FC = FF // P
TOKENS = SEQS * T
TILES = -(-TOKENS // P)
TAIL = TOKENS - (TILES - 1) * P
PAIRS = TILES + EXPERTS - 1
SLOTS = POS * SEQS
SHIFT = 64.0
EPS = 1e-5
BIG = 1e30
SPLIT = float((1 << 12) + 1)

f32 = mybir.dt.float32
bf16 = mybir.dt.bfloat16
f32r = mybir.dt.float32r
i32 = mybir.dt.int32
u32 = mybir.dt.uint32
ALU = mybir.AluOpType
ACT = mybir.ActivationFunctionType
AX = mybir.AxisListType


class Order:

    def __init__(self, eng, sem):
        self.eng, self.sem, self.base, self.n = eng, sem, 0, 0

    def link(self, ins):
        ins.then_inc(self.sem, 1)
        self.n += 1
        self.eng.wait_ge(self.sem, self.base + self.n)

    def enter(self, behind):
        self.outer, self.base, self.n = self.base + self.n, self.base + self.n + behind, 0

    def leave(self, turns, per_turn):
        assert self.n == per_turn, f"a turn has {self.n} steps, not {per_turn}"
        self.base, self.n = self.outer + turns * per_turn, 0


def moments(dve, order, stats, mean, spread, veps, sign=1.0):
    even, odd = stats[:, :, 1], stats[:, :, 4]
    dve.tensor_tensor(mean, even, odd, ALU.add)
    dve.tensor_tensor(spread, even, odd, ALU.subtract)
    order.link(dve.tensor_tensor(veps, stats[:, :, 2], stats[:, :, 5], ALU.add))
    dve.tensor_scalar(mean, mean, 0.5 * sign, None, ALU.mult)
    dve.tensor_tensor(spread, spread, spread, ALU.mult)
    order.link(dve.tensor_scalar(veps, veps, 1.0 / D, EPS, ALU.mult, ALU.add))
    return dve.scalar_tensor_tensor(out=veps, in0=spread, scalar=0.25, in1=veps,
                                    op0=ALU.mult, op1=ALU.add)


def build(nc, xT, tok_w, qkv_w, qkv_b, gate_w, gate_b, w1, b1, w2, b2, out):
    ctx = ExitStack()
    with ctx:
        def sb(name, shape, dt=f32, scope=ctx):
            return scope.enter_context(nc.sbuf_tensor(name, shape, dt))

        def pb(name, shape, dt=f32, scope=ctx):
            return scope.enter_context(nc.psum_tensor(name, shape, dt))

        def sem(name):
            return ctx.enter_context(nc.semaphore(name))

        ident = sb("ident", [P, P])
        half_neg = sb("half_neg", [P, SEQS])
        shift_col = sb("shift_col", [P, 1])
        h_all = sb("h_all", [P, POS, SEQS, D])
        qkvw_sb = sb("qkvw_sb", [P, QKV])
        qkvb_sb = sb("qkvb_sb", [P, QKV])
        gatew_sb = sb("gatew_sb", [P, EXPERTS])
        gateb_sb = sb("gateb_sb", [P, EXPERTS])
        w1_sb = sb("w1_sb", [P, EXPERTS, FF])
        w2_sb = sb("w2_sb", [P, EXPERTS, FC, D])
        b2_sb = sb("b2_sb", [P, EXPERTS, D])
        onehot = sb("onehot", [P, POS, SEQS, EXPERTS])
        valid = sb("valid", [P, 1])
        before = sb("before", [P, P])
        ones = sb("ones", [P, P])

        NUMBERS = PAIRS + TILES + EXPERTS + P + 2 * SLOTS
        nums = sb("nums", [P, NUMBERS])
        q_row = nums[:, 0:PAIRS]
        cut_row = nums[:, PAIRS + 1:PAIRS + TILES]
        e_row = nums[:, PAIRS + TILES:PAIRS + TILES + EXPERTS]
        p_row = nums[:, NUMBERS - 2 * SLOTS - P:NUMBERS - 2 * SLOTS]
        token_p = nums[:, NUMBERS - 2 * SLOTS:NUMBERS - SLOTS]
        token_slot = nums[:, NUMBERS - SLOTS:]
        p_col = token_p[:, 0:1]

        h_dram = nc.dram_tensor("h_rows", (TOKENS, D), f32).ap()
        xs_dram = nc.dram_tensor("expert_rows", (SLOTS * P, D), f32).ap()

        s_w = sem("weights_loaded")
        s_wx = sem("expert_weights_loaded")
        s_init = sem("constants_made")
        s_dve = sem("vector_order")
        s_pool = sem("gpsimd_order")
        s_nums = sem("numbers_made")

        rows = ctx.enter_context(ExitStack())
        nT_all = sb("nT_all", [P, SEQS, TP], scope=rows)
        n_aug = sb("n_aug", [P, SEQS, POS, D + 1], scope=rows)

        with ExitStack() as a:
            x_in = [sb(f"x_in{u}", [P, T_IN], scope=a) for u in range(2)]
            ints = sb("ints", [P, NUMBERS], i32, scope=a)
            tokw_sb = sb("tokw_sb", [P, WINDOW, QKV], scope=a)
            w_hi = sb("conv_w_hi", [P, WINDOW, QKV], f32r, scope=a)
            w_lo = sb("conv_w_lo", [P, WINDOW, QKV], f32r, scope=a)
            x_hi = [sb(f"x_hi{u}", [P, T_IN], f32r, scope=a) for u in range(2)]
            x_lo = [sb(f"x_lo{u}", [P, T_IN], f32r, scope=a) for u in range(2)]
            t_x, d_x = ([sb(f"{name}{u}", [P, T_IN], scope=a) for u in range(2)]
                        for name in ("split_t_x", "split_d_x"))
            t_w, d_w = (sb(name, [P, WINDOW, D], scope=a) for name in ("split_t_w", "split_d_w"))
            zt = [sb(f"zt{u}", [P, T], scope=a) for u in range(2)]
            ft = [sb(f"ft{u}", [P, T], scope=a) for u in range(2)]
            ot = [sb(f"ot{u}", [P, T], scope=a) for u in range(2)]
            fg = sb("forget", [P, T], scope=a)
            zin = sb("zin", [P, T], scope=a)
            cell = sb("cell", [P, T], scope=a)
            hT = [sb(f"hT{u}", [P, TP], scope=a) for u in range(2)]
            n_st = [sb(f"n_stage{u}", [P, POS, D], scope=a) for u in range(2)]
            stats = sb("stats_a", [P, POS, 6], scope=a)
            mean = sb("mean_a", [P, POS], scope=a)
            spread = sb("spread_a", [P, POS], scope=a)
            veps = sb("var_eps_a", [P, POS], scope=a)
            rstd = sb("rstd_a", [P, POS], scope=a)
            conv = pb("conv", [P, 3, 2, 512], scope=a)
            tr = pb("tr_a", [P, TP], scope=a)

            x_loaded = [sem("x_loaded_even"), sem("x_loaded_odd")]
            s_tokw = sem("conv_weights_loaded")
            t_ready, d_ready, hi_ready = sem("t_ready"), sem("d_ready"), sem("x_hi_ready")
            x_split, w_split = sem("x_split"), sem("conv_weights_split")
            conv_done, tanh_done = sem("conv_done"), sem("tanh_done")
            h_ready, hT_done, h_copied = sem("h_ready"), sem("h_transposed"), sem("h_copied")
            var_ready, rstd_ready = sem("var_ready_a"), sem("rstd_ready_a")
            n_ready, nT_done, nT_copied = sem("n_ready"), sem("n_transposed"), sem("nT_copied")
            n_kept = sem("n_kept")

            with nc.Block() as block:
                @block.sync
                def _(sp):
                    sp.dma_start(tokw_sb[:], tok_w).then_inc(s_tokw, 16)
                    for b in range(2):
                        sp.dma_start(x_in[b][:], xT[b]).then_inc(x_loaded[b], 16)
                    for dst, src in ((qkvw_sb, qkv_w), (gatew_sb, gate_w)):
                        sp.dma_start(dst[:], src).then_inc(s_w, 16)
                    sp.dma_start(qkvb_sb[:], qkv_b.partition_broadcast(P)).then_inc(s_w, 16)
                    sp.dma_start(gateb_sb[:], gate_b.partition_broadcast(P)).then_inc(s_w, 16)
                    with sp.Fori(2, SEQS - 1, 2) as b:
                        for u in range(2):
                            sp.wait_ge(x_split, b + u - 1)
                            sp.dma_start(x_in[u][:], xT[bass.ds(b + u, 1)].rearrange("o p t -> (o p) t")
                                         ).then_inc(x_loaded[u], 16)
                    for dst, src in ((w1_sb, w1), (w2_sb, w2)):
                        sp.dma_start(dst[:], src).then_inc(s_wx, 16)
                    sp.dma_start(b2_sb[:], b2.partition_broadcast(P)).then_inc(s_wx, 16)

                @block.gpsimd
                def _(pool):
                    order = Order(pool, s_pool)

                    def split_d(b, u):
                        pool.wait_ge(t_ready, b + 1)
                        pool.tensor_tensor(d_x[u][:], t_x[u][:], x_in[u][:],
                                           ALU.subtract).then_inc(d_ready, 1)

                    def split_lo(b, u):
                        pool.wait_ge(hi_ready, b + 1)
                        pool.tensor_tensor(x_lo[u][:], x_in[u][:], x_hi[u][:].bitcast(f32),
                                           ALU.subtract).then_inc(x_split, 1)

                    order.link(pool.memset(ident[:], 0.0))
                    pool.affine_select(out=ident[:], in_=ident[:], compare_op=ALU.not_equal, fill=1.0,
                                       base=0, pattern=[[-1, P]], channel_multiplier=1).then_inc(s_init, 1)
                    split_d(0, 0)
                    split_lo(0, 0)
                    order.link(pool.memset(ones[:], 1.0))
                    order.link(pool.affine_select(out=before[:], in_=ones[:], compare_op=ALU.is_gt,
                                                  fill=0.0, base=0, pattern=[[1, P]],
                                                  channel_multiplier=-1))
                    order.link(pool.affine_select(out=valid[:], in_=ones[:, 0:1], compare_op=ALU.is_gt,
                                                  fill=0.0, base=T_LAST, pattern=[[0, 1]],
                                                  channel_multiplier=-1))
                    order.link(pool.memset(half_neg[:], -0.5))
                    order.link(pool.memset(shift_col[:], -SHIFT))
                    order.link(pool.memset(n_aug[:, :, :, D], 1.0))
                    for l in range(SEQS):
                        order.link(pool.tensor_copy(n_aug[:, l, POS - 1, D:D + 1], valid[:]))

                    at0 = 0
                    for pattern, chan in (([[1, PAIRS]], 0), ([[P, TILES]], 0), ([[1, EXPERTS]], 0),
                                          ([[1, P]], 0), ([[0, SLOTS]], 1), ([[P, SLOTS]], 0)):
                        n = pattern[0][1]
                        pool.iota(ints[:, at0:at0 + n], pattern=pattern, base=0,
                                  channel_multiplier=chan).then_inc(s_nums, 1)
                        at0 += n

                    for b in (1, 2):
                        split_d(b, b % 2)
                        split_lo(b, b % 2)

                    def turn(b, u, split):
                        pool.wait_ge(var_ready, b + 1)
                        pool.tensor_tensor(rstd[:], veps[:], half_neg[:, 0:POS],
                                           ALU.pow).then_inc(rstd_ready, 1)
                        if split:
                            split_d(b + 3, 1 - u)
                        pool.wait_ge(n_ready, b + 1)
                        pool.tensor_copy(n_aug[:, bass.ds(b, 1), :, 0:D],
                                         n_st[u][:].rearrange("p (o j) d -> p o j d", o=1)
                                         ).then_inc(n_kept, 1)
                        if split:
                            split_lo(b + 3, 1 - u)

                    with pool.Fori(0, SEQS - 5, 2) as b:
                        for u in range(2):
                            turn(b + u, u, True)
                    for b in range(SEQS - 4, SEQS):
                        turn(b, b % 2, b + 3 < SEQS)

                @block.scalar
                def _(act):
                    def tanhs(b, u):
                        if not isinstance(b, int) or b >= 2:
                            act.wait_ge(h_ready, b - 1)
                        for g, (dst, scale) in enumerate(((zt[u], 1.0), (ft[u], 0.5), (ot[u], 0.5))):
                            act.wait_ge(conv_done, 3 * b + g + 1)
                            act.activation(dst[:].rearrange("p (h t) -> p h t", h=2),
                                           conv[:, g, :, 0:HALF], ACT.Tanh,
                                           scale=scale).then_inc(tanh_done, 1)

                    def keep_nT(b):
                        act.wait_ge(nT_done, b + 1)
                        act.activation(nT_all[:, bass.ds(b, 1), :].rearrange("p o t -> p (o t)"),
                                       tr[:], ACT.Copy).then_inc(nT_copied, 1)

                    def keep_h(b):
                        act.wait_ge(n_ready, b + 1)
                        act.activation(h_all[:, :, bass.ds(b, 1), :],
                                       tr[:].rearrange("p (j o d) -> p j o d", o=1, d=D),
                                       ACT.Copy).then_inc(h_copied, 1)

                    def split_t(b, u, loaded):
                        act.wait_ge(x_loaded[u], loaded)
                        if not isinstance(b, int) or b >= 2:
                            act.wait_ge(hi_ready, b - 1)
                        act.activation(t_x[u][:], x_in[u][:], ACT.Copy,
                                       scale=SPLIT).then_inc(t_ready, 1)

                    def turn(b, u, loaded=None):
                        tanhs(b + 1, 1 - u)
                        if loaded is not None:
                            split_t(b + 3, 1 - u, loaded)
                        keep_nT(b - 1)
                        keep_h(b)

                    split_t(0, 0, 16)
                    split_t(1, 1, 16)
                    tanhs(0, 0)
                    split_t(2, 0, 32)
                    tanhs(1, 1)
                    split_t(3, 1, 32)
                    keep_h(0)
                    with act.Fori(1, SEQS - 4, 2) as b:
                        turn(b, 1, 8 * b + 40)
                        turn(b + 1, 0, 8 * b + 40)
                    turn(SEQS - 3, 1)
                    turn(SEQS - 2, 0)
                    keep_nT(SEQS - 2)
                    keep_h(SEQS - 1)
                    keep_nT(SEQS - 1)

                @block.vector
                def _(dve):
                    order = Order(dve, s_dve)

                    def split_hi(b, u):
                        dve.wait_ge(d_ready, b + 1)
                        if not isinstance(b, int) or b >= 2:
                            dve.wait_ge(conv_done, 3 * b - 3)
                        dve.tensor_tensor(x_hi[u][:], t_x[u][:], d_x[u][:],
                                          ALU.subtract).then_inc(hi_ready, 1)

                    dve.wait_ge(s_tokw, 16)
                    for g in range(3):
                        cols = slice(g * D, (g + 1) * D)
                        w, hi, lo = tokw_sb[:, :, cols], w_hi[:, :, cols], w_lo[:, :, cols]
                        order.link(dve.tensor_scalar(t_w[:], w, SPLIT, None, ALU.mult))
                        order.link(dve.tensor_tensor(d_w[:], t_w[:], w, ALU.subtract))
                        order.link(dve.tensor_tensor(hi, t_w[:], d_w[:], ALU.subtract))
                        dve.tensor_tensor(lo, w, hi.bitcast(f32), ALU.subtract).then_inc(w_split, 1)
                        if g == 0:
                            split_hi(0, 0)
                    split_hi(1, 1)
                    for u in range(2):
                        order.link(dve.memset(hT[u][:, T:TP], 0.0))
                    dve.wait_ge(s_nums, 6)
                    order.link(dve.tensor_copy(nums[:], ints[:]))
                    for number in (token_p, token_slot):
                        order.link(dve.tensor_scalar(number[:, SLOTS - SEQS:], number[:, SLOTS - SEQS:],
                                                     valid[:], None, ALU.mult))

                    def recur(b, u):
                        dve.wait_ge(tanh_done, 3 * b + 2)
                        dve.tensor_scalar(fg[:], ft[u][:], 0.5, 0.5, ALU.mult, ALU.add)
                        order.link(dve.tensor_scalar(zin[:], ft[u][:], -0.25, 0.25, ALU.mult, ALU.add))
                        order.link(dve.tensor_tensor(zin[:], zin[:], zt[u][:], ALU.mult))
                        order.link(dve.tensor_tensor_scan(cell[:], fg[:], zin[:], 0.0,
                                                          ALU.mult, ALU.add))
                        dve.wait_ge(tanh_done, 3 * b + 3)
                        if not isinstance(b, int) or b >= 2:
                            dve.wait_ge(hT_done, b - 1)
                        dve.scalar_tensor_tensor(out=hT[u][:, 0:T], in0=ot[u][:], scalar=1.0,
                                                 in1=cell[:], op0=ALU.add,
                                                 op1=ALU.mult).then_inc(h_ready, 1)

                    def norm(b, u):
                        dve.wait_ge(hT_done, b + 1)
                        for j in range(POS):
                            last = dve.bn_stats(stats[:, j, :], tr[:, j * D:(j + 1) * D])
                        order.link(last)
                        moments(dve, order, stats, mean[:], spread[:], veps[:]).then_inc(var_ready, 1)
                        dve.wait_ge(rstd_ready, b + 1)
                        if not isinstance(b, int) or b >= 2:
                            dve.wait_ge(nT_done, b - 1)
                            dve.wait_ge(n_kept, b - 1)
                        for j in range(POS):
                            last = dve.tensor_scalar(n_st[u][:, j, :], tr[:, j * D:(j + 1) * D],
                                                     mean[:, j:j + 1], rstd[:, j:j + 1],
                                                     ALU.subtract, ALU.mult)
                        last.then_inc(n_ready, 1)

                    def turn(b, u):
                        recur(b + 1, 1 - u)
                        norm(b, u)

                    recur(0, 0)
                    split_hi(2, 0)
                    turn(0, 0)
                    split_hi(3, 1)
                    per = 2 * 6
                    with dve.Fori(1, SEQS - 4, 2) as b:
                        order.enter((b - 1) * (per // 2))
                        for n in range(2):
                            turn(b + n, 1 - n)
                            split_hi(b + n + 3, n)
                    order.leave((SEQS - 4) // 2, per)
                    turn(SEQS - 3, 1)
                    recur(SEQS - 1, 1)
                    norm(SEQS - 2, 0)
                    norm(SEQS - 1, 1)

                @block.tensor
                def _(pe):
                    pe.wait_ge(s_init, 1)

                    def convolve(b, u):
                        pe.wait_ge(x_split, b + 1)
                        for g in range(3):
                            if isinstance(b, int) and b == 0:
                                pe.wait_ge(w_split, g + 1)
                            if not isinstance(b, int) or b >= 1:
                                pe.wait_ge(tanh_done, 3 * b + g - 2)
                            for half in range(2):
                                for w in range(WINDOW):
                                    at = half * HALF + w
                                    for n, (wp, xp) in enumerate(((w_hi, x_hi), (w_hi, x_lo),
                                                                  (w_lo, x_hi))):
                                        last = pe.matmul(conv[:, g, half, 0:HALF],
                                                         wp[:, w, g * D:(g + 1) * D],
                                                         xp[u][:, at:at + HALF],
                                                         start=(w == 0 and n == 0),
                                                         stop=(w == WINDOW - 1 and n == 2))
                            last.then_inc(conv_done, 1)

                    def transpose_n(b, u):
                        pe.wait_ge(h_copied, b + 1)
                        for j in range(POS):
                            last = pe.transpose(tr[:, j * P:(j + 1) * P], n_st[u][:, j, :], ident[:])
                        last.then_inc(nT_done, 1)

                    def transpose_h(b, u):
                        pe.wait_ge(h_ready, b + 1)
                        if not isinstance(b, int) or b >= 1:
                            pe.wait_ge(nT_copied, b)
                        for j in range(POS):
                            last = pe.transpose(tr[:, j * P:(j + 1) * P],
                                                hT[u][:, j * P:(j + 1) * P], ident[:])
                        last.then_inc(hT_done, 1)

                    convolve(0, 0)
                    convolve(1, 1)
                    transpose_h(0, 0)
                    with pe.Fori(1, SEQS - 2, 2) as b:
                        for u in range(2):
                            convolve(b + u + 1, u)
                            transpose_n(b + u - 1, u)
                            transpose_h(b + u, 1 - u)
                    transpose_n(SEQS - 2, 0)
                    transpose_h(SEQS - 1, 1)
                    transpose_n(SEQS - 1, 1)

        with ExitStack() as b_:
            POOL_L = (1, 3, 5, 6, 7)
            OWN_AV = (0, 3)
            POOL_AV = tuple(l for l in range(SEQS) if l not in OWN_AV)
            PE_AV = (6, 7)
            DVE_AV = tuple(l for l in range(SEQS) if l not in PE_AV)
            expo = [sb(f"expo{u}", [P, POS, P], scope=b_) for u in range(2)]
            pv_sb = sb("pv_sb", [P, SEQS, D + 1], scope=b_)
            rec = sb("rec", [P, SEQS], scope=b_)
            h1 = sb("h1", [P, SEQS, D], scope=b_)
            h2 = sb("h2", [P, SEQS, D], scope=b_)
            nw = sb("n_work", [P, SEQS, D], scope=b_)
            h3 = sb("h3", [P, SEQS, D], scope=b_)
            n3 = sb("n3", [P, SEQS, D], scope=b_)
            nTw = sb("n_work_T", [P, SEQS, P], scope=b_)
            qkv = sb("qkv", [P, SEQS, QKV], scope=b_)
            prod = [sb(f"prod{u}", [P, HEADS, SEQS, HD], scope=b_) for u in range(4)]
            nbias = sb("minus_mean_rstd", [P, SEQS], scope=b_)
            prodp = [sb(f"prod_pool{u}", [P, HEADS, SEQS, HD], scope=b_) for u in range(2)]
            scores = sb("scores", [P, SEQS, HEADS, SEQS], scope=b_)
            probs = sb("probs", [P, SEQS, HEADS, SEQS], scope=b_)
            top = sb("top", [P, SEQS, HEADS], scope=b_)
            alive = sb("alive", [P, SEQS, HEADS], scope=b_)
            att = sb("att", [P, SEQS - len(PE_AV), D], scope=b_)
            statsb = sb("stats_b", [P, SEQS, 6], scope=b_)
            meanb = sb("mean_b", [P, SEQS], scope=b_)
            spreadb = sb("spread_b", [P, SEQS], scope=b_)
            vepsb = sb("var_eps_b", [P, SEQS], scope=b_)
            rstdb = sb("rstd_b", [P, SEQS], scope=b_)
            logit = sb("logit", [P, SEQS, EXPERTS], scope=b_)
            elog = sb("exp_logit", [P, SEQS, EXPERTS], scope=b_)
            mxl = sb("max_logit", [P, SEQS], scope=b_)
            pmax = sb("pmax", [P, SEQS], scope=b_)
            best = sb("best", [P, SEQS, EXPERTS], scope=b_)
            firstw = sb("first_weight", [P, EXPERTS], scope=b_)
            s_ps = [pb(f"scores_ps{u}", [P, 1024], scope=b_) for u in range(2)]
            pv_ps = [pb(f"pv_ps{u}", [P, 512], scope=b_) for u in range(2)]
            t_ps = [pb(f"t_ps{u}", [P, 512], scope=b_) for u in range(2)]
            g_ps = pv_ps[0]

            def q_ps(l):
                return s_ps[l // 2 % 2][:, l % 2 * 512:l % 2 * 512 + QKV]

            s_dveb = sem("vector_order_b")
            s_done, exp_done = sem("nn_done"), sem("exp_done")
            pv_done, pv_copied, pv_read = sem("pv_done"), sem("pv_copied"), sem("pv_read")
            varb_ready, rstdb_ready = sem("var_ready_b"), sem("rstd_ready_b")
            n2_ready, n3_ready = sem("n2_ready"), sem("n3_ready")
            t_done, t_copied = sem("t_done"), sem("t_copied")
            q_done, q_read = sem("qkv_done"), sem("qkv_read")
            g_done, g_read = sem("gate_done"), sem("gate_read")
            sm_ready, sm_done = sem("head_scores_ready"), sem("head_exp_done")
            probs_ready, av_ready, av_read = sem("probs_ready"), sem("av_ready"), sem("av_read")
            av_summed = sem("av_summed")
            n1_ready, xs_ready = sem("n1_ready"), sem("expert_rows_ready")
            rec_ready, h1_ready = sem("rec_ready"), sem("h1_ready")
            h2_ready, h2_kept = sem("h2_ready"), sem("h2_kept")
            scp_ready, scp_read = sem("pool_scores_ready"), sem("pool_scores_read")
            s_poolb = sem("gpsimd_order_b")
            h3_ready, h3_stored = sem("h3_ready"), sem("h3_stored")
            xs_stored = sem("expert_rows_stored")
            lg_ready, lg_done = sem("logits_ready"), sem("logits_exp_done")
            pmax_ready, q_scaled = sem("pmax_ready"), sem("q_weights_scaled")

            def known(v):
                return isinstance(v, int)

            def at(v):
                return bass.ds(v, 1)

            ALL = SEQS * POS

            def upto(v, most):
                return min(v, most) if known(v) else v

            def t_before_project(i):
                return 4 * i - 2 if not known(i) or i else 0

            def t_before_gate(i):
                return upto(4 * i + 4, 4 * POS - 2)

            def ln_last(i):
                return upto(3 * i + 2, 3 * POS)

            def ln_first(i):
                return 3 * i + 3

            def schedule(turn, loop):
                turn(0)
                with loop(1, POS - 2) as i:
                    turn(i)
                turn(POS - 2)
                turn(POS - 1)

            def more(i, ahead):
                return not known(i) or i + ahead < POS

            def later(i):
                return not known(i) or i >= 1

            with nc.Block() as block:
                @block.tensor
                def _(pe):
                    def self_attention(i):
                        def nn(l):
                            if not (known(i) and i == 0 and l < 2):
                                pe.wait_ge(exp_done, SEQS * i + l - 1)
                            for j in range(POS):
                                last = pe.matmul(s_ps[l % 2][:, j * P:(j + 1) * P],
                                                 nT_all[:, l, j * P:(j + 1) * P],
                                                 nT_all[:, l, bass.ds(i * P, P)], start=True, stop=True)
                            last.then_inc(s_done, 1)

                        def pv(l):
                            pe.wait_ge(exp_done, SEQS * i + l + 1)
                            if not (known(i) and i == 0 and l < 2):
                                pe.wait_ge(pv_copied, SEQS * i + l - 1)
                            for j in range(POS):
                                last = pe.matmul(pv_ps[l % 2][:, 0:D + 1], expo[l % 2][:, j, :],
                                                 n_aug[:, l, j, :], start=(j == 0), stop=(j == POS - 1))
                            last.then_inc(pv_done, 1)

                        nn(0)
                        for l in range(1, SEQS):
                            nn(l)
                            pv(l - 1)
                        pv(SEQS - 1)

                    def transpose_4(src, group, t_before):
                        if not known(t_before) or t_before + group > 1:
                            pe.wait_ge(t_copied, t_before + group - 1)
                        for m in range(4):
                            last = pe.transpose(t_ps[group][:, m * P:(m + 1) * P],
                                                src[:, 4 * group + m, :], ident[:])
                        last.then_inc(t_done, 1)

                    def gate(i):
                        pe.wait_ge(n3_ready, i + 1)
                        for group in range(2):
                            transpose_4(n3, group, t_before_gate(i))
                        pe.wait_ge(t_copied, t_before_gate(i) + 2)
                        pe.wait_ge(pv_copied, upto(SEQS * (i + 4), ALL))
                        for l in range(SEQS):
                            last = pe.matmul(g_ps[:, l * EXPERTS:(l + 1) * EXPERTS], nTw[:, l, :],
                                             gatew_sb[:], start=True, stop=True)
                        last.then_inc(g_done, 1)

                    def value_sums(i):
                        for n, l in enumerate(PE_AV):
                            at_n = POOL_AV.index(l)
                            product = prod[at_n % 4]
                            pe.wait_ge(av_ready, len(POOL_AV) * i + at_n + 1)
                            for m in range(SEQS):
                                last = pe.matmul(t_ps[1][:, n * D:(n + 1) * D].rearrange(
                                    "p (h c) -> p h c", c=HD), ident[:], product[:, :, m, :],
                                    start=(m == 0), stop=(m == SEQS - 1))
                            last.then_inc(av_summed, 1)

                    def project(i):
                        pe.wait_ge(n2_ready, i + 1)
                        for group in range(2):
                            transpose_4(nw, group, t_before_project(i))
                        pe.wait_ge(t_copied, t_before_project(i) + 2)
                        pe.wait_ge(exp_done, upto(SEQS * (i + 2), ALL))
                        if later(i):
                            pe.wait_ge(q_read, SEQS * i)
                        for l in range(SEQS):
                            if l == 4 and later(i):
                                value_sums(i - 1)
                            if l >= 4:
                                pe.wait_ge(q_read, SEQS * i + l - 3)
                            pe.matmul(q_ps(l), nTw[:, l, :], qkvw_sb[:],
                                      start=True, stop=True).then_inc(q_done, 1)

                    def turn(i):
                        if more(i, 2):
                            pe.wait_ge(q_read, SEQS * (i + 1))
                            if later(i):
                                pe.wait_ge(g_read, i)
                            self_attention(i + 2)
                        if later(i):
                            gate(i - 1)
                        if more(i, 1):
                            project(i + 1)
                        else:
                            value_sums(i)

                    self_attention(0)
                    self_attention(1)
                    pe.wait_ge(q_scaled, 2)
                    project(0)
                    schedule(turn, pe.Fori)
                    pe.wait_ge(g_read, POS)
                    gate(POS - 1)

                @block.scalar
                def _(act):
                    def self_attention(i, between=None):
                        for l in range(SEQS + 1):
                            if l < SEQS:
                                act.wait_ge(s_done, SEQS * i + l + 1)
                                if not known(i) or SEQS * i + l >= 2:
                                    act.wait_ge(pv_done, SEQS * i + l - 1)
                                act.activation(expo[l % 2][:].rearrange("p a b -> p (a b)"),
                                               s_ps[l % 2][:, 0:TP], ACT.Exp,
                                               bias=shift_col[:]).then_inc(exp_done, 1)
                            if l == 1 and later(i):
                                act.wait_ge(pv_read, i)
                            if l >= 1:
                                act.wait_ge(pv_done, SEQS * i + l)
                                act.activation(pv_sb[:, l - 1, :], pv_ps[(l - 1) % 2][:, 0:D + 1],
                                               ACT.Copy).then_inc(pv_copied, 1)
                            if between and l in between:
                                between[l]()

                    def copy_t(t_before, group):
                        act.wait_ge(t_done, t_before + group + 1)
                        act.activation(nTw[:, 4 * group:4 * group + 4, :].rearrange("p a b -> p (a b)"),
                                       t_ps[group][:], ACT.Copy).then_inc(t_copied, 1)

                    def apply(src, dst, n, ready):
                        act.wait_ge(rstdb_ready, n)
                        for l in range(SEQS):
                            last = act.activation(dst[:, l, :], src[:, l, :], ACT.Identity,
                                                  bias=nbias[:, l:l + 1], scale=rstdb[:, l:l + 1])
                        last.then_inc(ready, 1)

                    def norm_h1(i):
                        if later(i):
                            act.wait_ge(t_done, t_before_project(i - 1) + 2)
                        apply(h1, nw, ln_first(i - 1) if later(i) else 1, n1_ready)

                    def norm_h2(i):
                        apply(h2, nw, ln_first(i - 1) + 1 if later(i) else 2, n2_ready)

                    def norm_h3(i):
                        act.wait_ge(xs_ready, i + 1)
                        apply(h3, n3, upto(3 * i + 5, 3 * POS), n3_ready)

                    def head_exp(i):
                        act.wait_ge(sm_ready, i + 1)
                        act.activation(probs[:], probs[:], ACT.Exp).then_inc(sm_done, 1)

                    def gate_copies(i):
                        act.wait_ge(q_done, upto(SEQS * (i + 2), ALL))
                        for group in range(2):
                            copy_t(t_before_gate(i), group)

                    def project_copies(i):
                        for group in range(2):
                            copy_t(t_before_project(i), group)

                    def gate_exp(i):
                        act.wait_ge(lg_ready, i + 1)
                        act.activation(elog[:], logit[:], ACT.Exp).then_inc(lg_done, 1)

                    def expert_rows(i):
                        act.wait_ge(pmax_ready, i + 1)
                        act.wait_ge(h3_ready, i + 1)
                        for l in range(SEQS):
                            last = act.activation(
                                h_all[:, at(i), l, :].rearrange("p o d -> p (o d)"), n3[:, l, :],
                                ACT.Copy, scale=pmax[:, l:l + 1])
                        last.then_inc(xs_ready, 1)

                    def keep_h2(i):
                        act.wait_ge(h2_ready, i + 1)
                        act.activation(h_all[:, at(i)].rearrange("p o l d -> p (o l) d"), h2[:],
                                       ACT.Copy).then_inc(h2_kept, 1)

                    def turn(i):
                        woven = {8: lambda: head_exp(i)}
                        if later(i):
                            woven[1] = lambda: norm_h3(i - 1)
                        if more(i, 1):
                            woven[3] = lambda: norm_h1(i + 1)
                        if more(i, 2):
                            self_attention(i + 2, woven)
                        else:
                            for l in sorted(woven):
                                woven[l]()
                        if later(i):
                            gate_copies(i - 1)
                        if more(i, 1):
                            norm_h2(i + 1)
                            keep_h2(i + 1)
                            project_copies(i + 1)
                        if later(i):
                            gate_exp(i - 1)
                            expert_rows(i - 1)

                    self_attention(0)
                    self_attention(1, {4: lambda: norm_h1(0), 7: lambda: norm_h2(0)})
                    keep_h2(0)
                    project_copies(0)
                    schedule(turn, act.Fori)
                    norm_h3(POS - 1)
                    gate_copies(POS - 1)
                    gate_exp(POS - 1)
                    expert_rows(POS - 1)

                @block.gpsimd
                def _(pool):
                    order = Order(pool, s_poolb)
                    heads = qkv[:].rearrange("p m (h c) -> p h m c", c=3 * HD)
                    key_rows, value_rows = heads[:, :, :, HD:2 * HD], heads[:, :, :, 2 * HD:]

                    def rstd_of(n, used=None, times=0):
                        if used:
                            pool.wait_ge(used, times)
                        pool.wait_ge(varb_ready, n)
                        order.link(pool.tensor_tensor(rstdb[:], vepsb[:], half_neg[:], ALU.pow))
                        pool.tensor_tensor(nbias[:], meanb[:], rstdb[:], ALU.mult
                                           ).then_inc(rstdb_ready, 1)

                    def unnormed(i):
                        pool.wait_ge(rec_ready, i + 1)
                        if later(i):
                            pool.wait_ge(h2_ready, i)
                        pool.tensor_tensor(h1[:], pv_sb[:, :, 0:D],
                                           rec[:].unsqueeze(2).broadcast_to([P, SEQS, D]),
                                           ALU.mult).then_inc(pv_read, 1)

                    def residual(i):
                        pool.wait_ge(pv_read, i + 1)
                        order.link(pool.tensor_tensor(h1[:], h1[:], n_aug[:, :, at(i), 0:D].rearrange(
                            "p l o d -> p (l o) d"), ALU.mult))
                        pool.tensor_tensor(h1[:], h1[:], h_all[:, at(i)].rearrange(
                            "p o l d -> p (o l) d"), ALU.add).then_inc(h1_ready, 1)

                    def score_product(i, n):
                        reads = len(POOL_L) * i + n - 2
                        if not known(reads) or reads >= 0:
                            pool.wait_ge(scp_read, reads + 1)
                        query = heads[:, :, POOL_L[n], 0:HD].unsqueeze(2).broadcast_to(
                            [P, HEADS, SEQS, HD])
                        pool.tensor_tensor(prodp[n % 2][:], query, key_rows, ALU.mult
                                           ).then_inc(scp_ready, 1)

                    def turn(i):
                        if more(i, 1):
                            unnormed(i + 1)
                            residual(i + 1)
                        pool.wait_ge(q_read, SEQS * (i + 1))
                        for n in range(len(POOL_L)):
                            score_product(i, n)
                            if n == 0 and later(i):
                                rstd_of(ln_last(i), n2_ready, i + 1)
                            if n == 1 and more(i, 1):
                                if later(i):
                                    rstd_of(ln_first(i), n3_ready, i)
                                else:
                                    rstd_of(ln_first(i), n2_ready, 1)
                        if more(i, 1):
                            rstd_of(ln_first(i) + 1, n1_ready, i + 2)
                        pool.wait_ge(probs_ready, i + 1)
                        for n, l in enumerate(POOL_AV):
                            before_l = POOL_AV[n - 4]
                            if n >= 4 and before_l in PE_AV:
                                pool.wait_ge(av_summed, len(PE_AV) * i + PE_AV.index(before_l) + 1)
                            elif n >= 4:
                                pool.wait_ge(av_read, len(DVE_AV) * i + DVE_AV.index(before_l) + 1)
                            pool.tensor_tensor(
                                prod[n % 4][:],
                                probs[:, l, :, :].unsqueeze(3).broadcast_to([P, HEADS, SEQS, HD]),
                                value_rows, ALU.mult).then_inc(av_ready, 1)

                    unnormed(0)
                    residual(0)
                    rstd_of(1)
                    rstd_of(2, n1_ready, 1)
                    turn(0)
                    with pool.Fori(1, POS - 2) as i:
                        order.enter((i - 1) * 4)
                        turn(i)
                    order.leave(POS - 3, 4)
                    turn(POS - 2)
                    turn(POS - 1)
                    rstd_of(3 * POS, n3_ready, POS - 1)

                @block.sync
                def _(sp):
                    h_rows = h_dram.rearrange("(l t) d -> t l d", l=SEQS)
                    expert_rows = xs_dram.rearrange("(i l p) d -> p i l d", i=POS, l=SEQS)

                    def store_h(i, n=P):
                        sp.wait_ge(h3_ready, i + 1)
                        sp.dma_start(h_rows[bass.ds(i * P, n)], h3[0:n]).then_inc(h3_stored, 16)

                    def store_expert_rows(i):
                        sp.wait_ge(xs_ready, i + 2)
                        sp.dma_start(expert_rows[:, at(i)], h_all[:, at(i)]
                                     ).then_inc(xs_stored, 16)

                    store_h(0)
                    with sp.Fori(1, POS - 1) as i:
                        store_h(i)
                        store_expert_rows(i - 1)
                    store_h(POS - 1, T_LAST)
                    store_expert_rows(POS - 2)
                    store_expert_rows(POS - 1)
                    sp.wait_ge(h3_stored, 16 * POS)

                @block.vector
                def _(dve):
                    order = Order(dve, s_dveb)
                    for e in range(EXPERTS):
                        last = dve.memset(firstw[:, e:e + 1], float(EXPERTS - e))
                    order.link(last)
                    dve.wait_ge(s_w, 64)
                    for t in (qkvw_sb, qkvb_sb):
                        q_part = t[:].rearrange("p (h c) -> p h c", c=3 * HD)[:, :, 0:HD]
                        dve.tensor_scalar(q_part, q_part, HD ** -0.5, None,
                                          ALU.mult).then_inc(q_scaled, 1)

                    def wide(col, n):
                        return col.unsqueeze(2).broadcast_to([P, SEQS, n])

                    def row_stats(src, n):
                        for l in range(SEQS):
                            last = dve.bn_stats(statsb[:, l, :], src[:, l, :])
                        order.link(last)
                        row_moments(n)

                    def row_moments(n):
                        if not known(n) or n >= 2:
                            dve.wait_ge(rstdb_ready, n - 1)
                        moments(dve, order, statsb, meanb[:], spreadb[:], vepsb[:], sign=-1.0
                                ).then_inc(varb_ready, 1)

                    def sums(i):
                        dve.wait_ge(pv_copied, SEQS * (i + 1))
                        dve.reciprocal(rec[:], pv_sb[:, :, D]).then_inc(rec_ready, 1)

                    def stats_h1(i, n):
                        dve.wait_ge(h1_ready, i + 1)
                        row_stats(h1, n)

                    def second_residual(i, n):
                        if later(i):
                            dve.wait_ge(h2_kept, i)
                        dve.wait_ge(n1_ready, i + 1)
                        dve.tensor_tensor(h2[:], h1[:], nw[:], ALU.add).then_inc(h2_ready, 1)
                        dve.wait_ge(h2_ready, i + 1)
                        row_stats(h2, n)

                    def head_scores(i):
                        if more(i, 1):
                            sums(i + 1)
                        for l in range(SEQS):
                            dve.wait_ge(q_done, SEQS * i + l + 1)
                            dve.tensor_tensor(qkv[:, l, :], q_ps(l), qkvb_sb[:],
                                              ALU.add).then_inc(q_read, 1)
                            if later(i):
                                last = dve.bn_stats(statsb[:, l, :], h3[:, l, :])
                        if later(i):
                            order.link(last)
                            row_moments(ln_last(i))
                        dve.wait_ge(q_read, SEQS * (i + 1))
                        heads = qkv[:].rearrange("p m (h c) -> p h m c", c=3 * HD)
                        for l in range(SEQS):
                            if l in POOL_L:
                                n = POOL_L.index(l)
                                dve.wait_ge(scp_ready, len(POOL_L) * i + n + 1)
                                dve.tensor_reduce(scores[:, l], prodp[n % 2][:], AX.X, ALU.add
                                                  ).then_inc(scp_read, 1)
                            else:
                                query = heads[:, :, l, 0:HD].unsqueeze(2).broadcast_to(
                                    [P, HEADS, SEQS, HD])
                                own = l // 2 % 2
                                order.link(dve.tensor_tensor(prod[own][:], query,
                                                             heads[:, :, :, HD:2 * HD], ALU.mult))
                                order.link(dve.tensor_reduce(scores[:, l], prod[own][:], AX.X, ALU.add))
                            if l == 1 and more(i, 1):
                                stats_h1(i + 1, ln_first(i))
                            if l == 6 and more(i, 1):
                                second_residual(i + 1, ln_first(i) + 1)
                        dve.wait_ge(scp_read, len(POOL_L) * (i + 1))

                    def head_softmax(i):
                        flat = "p l h m -> p (l h) m"
                        sc, pr = (x[:].rearrange(flat) for x in (scores, probs))
                        tp, al = (x[:].rearrange("p l h -> p (l h)") for x in (top, alive))
                        tpw = tp.unsqueeze(2).broadcast_to([P, SEQS * HEADS, SEQS])
                        order.link(dve.tensor_scalar(pr, sc, 0.0, -BIG, ALU.is_equal, ALU.mult))
                        order.link(dve.tensor_tensor(pr, sc, pr, ALU.add))
                        order.link(dve.tensor_reduce(tp, pr, AX.X, ALU.max))
                        dve.tensor_tensor(pr, pr, tpw, ALU.subtract).then_inc(sm_ready, 1)
                        order.link(dve.tensor_scalar(al, tp, -0.5 * BIG, None, ALU.is_gt))
                        dve.wait_ge(sm_done, i + 1)
                        order.link(dve.tensor_reduce(tp, pr, AX.X, ALU.add))
                        order.link(dve.reciprocal(tp, tp))
                        order.link(dve.tensor_tensor(tp, tp, al, ALU.mult))
                        dve.tensor_tensor(pr, pr, tpw, ALU.mult).then_inc(probs_ready, 1)

                    def head_values(i):
                        heads = qkv[:].rearrange("p m (h c) -> p h m c", c=3 * HD)
                        for n, l in enumerate(DVE_AV):
                            if l in OWN_AV:
                                dve.wait_ge(probs_ready, i + 1)
                                weight = probs[:, l, :, :].unsqueeze(3).broadcast_to(
                                    [P, HEADS, SEQS, HD])
                                product = prodp[OWN_AV.index(l) % 2]
                                order.link(dve.tensor_tensor(product[:], weight,
                                                             heads[:, :, :, 2 * HD:], ALU.mult))
                            else:
                                at_n = POOL_AV.index(l)
                                product = prod[at_n % 4]
                                dve.wait_ge(av_ready, len(POOL_AV) * i + at_n + 1)
                            dve.tensor_reduce(att[:, n, :].rearrange("p (h c) -> p h c", c=HD),
                                              product[:].rearrange("p h m c -> p h c m"),
                                              AX.X, ALU.add).then_inc(av_read, 1)
                        dve.wait_ge(av_read, len(DVE_AV) * (i + 1))

                    def third_residual(i):
                        if later(i):
                            dve.wait_ge(h3_stored, 16 * i)
                            dve.wait_ge(n3_ready, i)
                        dve.wait_ge(h2_kept, i + 1)
                        h2_tile = h_all[:, at(i)].rearrange("p o l d -> p (o l) d")
                        split = len(DVE_AV)
                        dve.tensor_tensor(h3[:, 0:split], h2_tile[:, 0:split], att[:], ALU.add)
                        dve.wait_ge(av_summed, len(PE_AV) * (i + 1))
                        sums_ps = t_ps[1][:, 0:len(PE_AV) * D].rearrange("p (l d) -> p l d", d=D)
                        dve.tensor_tensor(h3[:, split:], h2_tile[:, split:], sums_ps,
                                          ALU.add).then_inc(h3_ready, 1)
                        dve.wait_ge(h3_ready, i + 1)

                    def route(i):
                        dve.wait_ge(g_done, i + 1)
                        dve.tensor_tensor(
                            logit[:], g_ps[:, 0:SEQS * EXPERTS].rearrange("p (l e) -> p l e", e=EXPERTS),
                            gateb_sb[:].unsqueeze(1).broadcast_to([P, SEQS, EXPERTS]),
                            ALU.add).then_inc(g_read, 1)
                        dve.wait_ge(g_read, i + 2)
                        oh = onehot[:, at(i)].rearrange("p o l e -> p (o l) e")
                        order.link(dve.tensor_reduce(mxl[:], logit[:], AX.X, ALU.max))
                        order.link(dve.tensor_tensor(best[:], logit[:], wide(mxl[:], EXPERTS),
                                                     ALU.is_equal))
                        dve.tensor_tensor(logit[:], logit[:], wide(mxl[:], EXPERTS),
                                          ALU.subtract).then_inc(lg_ready, 1)
                        order.link(dve.tensor_tensor(
                            best[:], best[:], firstw[:].unsqueeze(1).broadcast_to([P, SEQS, EXPERTS]),
                            ALU.mult))
                        order.link(dve.tensor_reduce(mxl[:], best[:], AX.X, ALU.max))
                        order.link(dve.tensor_tensor(oh, best[:], wide(mxl[:], EXPERTS), ALU.is_equal))
                        if known(i) and i == POS - 1:
                            dve.tensor_scalar(oh, oh, valid[:], None, ALU.mult)
                        dve.wait_ge(lg_done, i + 1)
                        order.link(dve.tensor_reduce(mxl[:], elog[:], AX.X, ALU.add))
                        if later(i):
                            dve.wait_ge(xs_ready, i + 1)
                        dve.reciprocal(pmax[:], mxl[:]).then_inc(pmax_ready, 1)

                    def turn(i):
                        head_scores(i)
                        head_softmax(i)
                        head_values(i)
                        if later(i):
                            route(i - 1)
                        third_residual(i)

                    dve.memset(logit[:], 0.0).then_inc(g_read, 1)
                    dve.memset(best[:], 0.0).then_inc(xs_ready, 1)
                    sums(0)
                    stats_h1(0, 1)
                    second_residual(0, 2)
                    turn(0)
                    per = 30
                    with dve.Fori(1, POS - 2) as i:
                        order.enter((i - 1) * per)
                        turn(i)
                    order.leave(POS - 3, per)
                    turn(POS - 2)
                    turn(POS - 1)
                    row_stats(h3, 3 * POS)
                    route(POS - 1)

        rows.close()
        with ExitStack() as c_:
            def sc(name, shape, dt=f32):
                return sb(name, shape, dt, scope=c_)

            ROUND = 1.5 * (1 << 23)
            GROUP = 4
            BACK = 3
            SPAN = BACK + GROUP
            END = PAIRS + BACK
            EXP_BITS, TILE_BITS = 3, 6
            WORDS = END + GROUP
            experts_of = sc("experts_of", [P, WORDS], i32)
            tiles_of = sc("tiles_of", [P, WORDS], i32)
            owned = sc("owned", [P, PAIRS])
            total = sc("total", [P, EXPERTS, SEQS, POS])
            upto = sc("upto", [P, EXPERTS, SEQS, POS])
            below = sc("below", [P, EXPERTS, SEQS, POS])
            ones_row = sc("ones_row", [P, EXPERTS * SLOTS])
            spot = sc("spot", [P, POS, SEQS, EXPERTS])
            place = sc("place", [P, SLOTS])
            place_k = sc("place_k", [P, SLOTS])
            place_r = sc("place_r", [P, SLOTS])
            hot_r = sc("hot_r", [P, SLOTS, P], bf16)
            is_k = sc("is_k", [P, SLOTS, TILES], bf16)
            hot_k = sc("hot_k", [P, SLOTS, 2, TILES], bf16)
            source = sc("source", [P, TILES], u32)
            ends = sc("ends", [P, 4, EXPERTS])
            start, stop, jump, last_tile = (ends[:, n, :] for n in range(4))
            count = sc("pair_count", [P, EXPERTS])
            cincl = sc("pairs_upto", [P, EXPERTS])
            cuts = sc("cuts", [P, EXPERTS, TILES - 1])
            sel = sc("sel", [P, PAIRS, EXPERTS])
            tmp = sc("sel_times", [P, PAIRS, EXPERTS])
            exp_line = sc("expert_line", [P, WORDS + SPAN - 1])
            tile_line = sc("tile_line", [P, WORDS + SPAN - 1])
            expf = exp_line[:, BACK:BACK + PAIRS]
            tilef = tile_line[:, BACK:BACK + PAIRS]
            packed = [sc(f"packed{u}", [P, WORDS]) for u in range(2)]
            first_row = sc("first_row", [P, PAIRS])
            stop_row = sc("stop_row", [P, PAIRS])
            row = sc("row", [P, PAIRS])

            y = sc("y", [P, TILES, D])
            b1_sb = sc("b1_sb", [P, EXPERTS, FF])
            x_sorted = h_all[:].rearrange("p i l d -> p (i l) d")
            x_rows = [sc(f"x_rows{u}", [P, D]) for u in range(2)]
            xTd = [sc(f"xT_sorted{u}", [P, P]) for u in range(2)]
            hid = [sc(f"hidden{u}", [P, FF]) for u in range(2)]
            hidT = [sc(f"hidden_T{u}", [P, FC, P]) for u in range(2)]
            yb = sc("y_bias", [P, D])
            x_ps = pb("x_ps", [P, 512], scope=c_)
            hid_ps = [pb(f"hid_ps{u}", [P, FF], scope=c_) for u in range(2)]
            hT_ps = [pb(f"hT_ps{u}", [P, 512], scope=c_) for u in range(2)]
            y_ps = [pb(f"y_ps{u}", [P, 512], scope=c_) for u in range(2)]
            before_ps, total_ps, source_ps = hid_ps[0], hid_ps[1], y_ps[0]

            s_cnt, is_k_made = sem("counted"), sem("is_k_made")
            r_made, k_made = sem("one_hot_r_made"), sem("one_hot_k_made")
            s_inv, s_source = sem("sources_summed"), sem("sources_ready")
            s_pairs, s_dvec, s_poolc = sem("pairs_listed"), sem("vector_order_c"), sem("gpsimd_order_c")
            b1_loaded = sem("b1_loaded")
            y_loaded, s_out = sem("h_rows_loaded"), sem("out_stored")
            gathered = [sem(f"rows_gathered{u}") for u in range(GROUP)]
            x_staged = sem("x_rows_staged")
            x_done, xT_ready = sem("x_transposed"), sem("xT_ready")
            up_done, hid_ready = sem("up_done"), sem("hidden_ready")
            hT_done2, hidT_ready = sem("hidden_transposed"), sem("hidden_T_ready")
            down_done, y_read, y_added = sem("down_done"), sem("y_read"), sem("y_added")
            LAG = EXPERTS

            def is_int(v):
                return isinstance(v, int)

            def steps(step, loop, words=None):
                first, stop, body = 3 * GROUP, TILES // GROUP * GROUP, 2 * GROUP
                assert (stop - first) % body == 0

                def turn(t, n=GROUP):
                    word = words(t) if words else None
                    for u in range(n):
                        step(t + u, u, word)

                for t in range(0, first, GROUP):
                    turn(t)
                with loop(first, stop - body + 1, body) as t:
                    turn(t)
                    turn(t + GROUP)
                for t in range(stop, END, GROUP):
                    turn(t, min(GROUP, END - t))

            def packed_words(eng, table, bits, n):
                return lambda t: eng.value_load(table[0:1, bass.ds(t, 1)], min_val=0,
                                                max_val=(1 << bits * n) - 1)

            BOUNDED = "the packed lines are bounded above by EXPERTS - 1 and TILES - 1"

            def entry(eng, word, bits, k, top):
                value = eng.snap((word >> (bits * k)) & ((1 << bits) - 1))
                return nc.s_assert_within(value, 0, top, skip_runtime_bounds_check_because=BOUNDED)

            with nc.Block() as block:
                @block.sync
                def _(sp):
                    sp.dma_start(b1_sb[:], b1.partition_broadcast(P)).then_inc(b1_loaded, 16)
                    sp.dma_start(y[:, 0:TILES - 1, :], h_dram[0:(TILES - 1) * P].rearrange(
                        "(k p) d -> p k d", p=P)).then_inc(y_loaded, 16)
                    sp.wait_ge(s_poolc, 1)
                    sp.dma_start(y[0:TAIL, TILES - 1, :], h_dram[(TILES - 1) * P:TOKENS]
                                 ).then_inc(y_loaded, 16)
                    out_tiles = out[0:(TILES - 1) * P].rearrange("(k p) d -> p k d", p=P)
                    with sp.Fori(LAG, PAIRS) as q:
                        sp.wait_ge(y_added, q + 1)
                        sp.dma_start(out_tiles[:, bass.ds(q - LAG, 1), :],
                                     y[:, bass.ds(q - LAG, 1), :]).then_inc(s_out, 16)
                    sp.dma_start(out[(TILES - 1) * P:TOKENS], y[0:TAIL, TILES - 1, :]).then_inc(s_out, 16)
                    sp.wait_ge(s_out, 16 * TILES)

                @block.gpsimd
                def _(pool):
                    pool.memset(y[:, TILES - 1, :], 0.0).then_inc(s_poolc, 1)
                    for i in range(POS):
                        part = slice(i * SEQS, (i + 1) * SEQS)
                        pool.wait_ge(is_k_made, i + 1)
                        for n, number in enumerate((token_p, token_slot)):
                            last = pool.tensor_tensor(
                                hot_k[:, part, n, :], is_k[:, part, :],
                                number[:, part].unsqueeze(2).broadcast_to([P, SEQS, TILES]), ALU.mult)
                        last.then_inc(k_made, 1)
                    pool.wait_ge(s_source, 1)
                    pool.wait_ge(xs_stored, 16 * POS)
                    for k in range(TILES):
                        u = k % GROUP
                        if k >= GROUP:
                            pool.wait_ge(gathered[u], 16 * (k // GROUP))
                        pool.indirect_dma_start(
                            x_sorted[:, k, :], None, xs_dram[:, :],
                            bass.IndirectOffsetOnAxis(ap=source[:, k:k + 1], axis=0),
                            bounds_check=SLOTS * P - 1, oob_is_err=False).then_inc(gathered[u], 16)

                @block.tensor
                def _(pe):
                    flat = onehot[:].rearrange("p i l e -> p (i l e)")
                    pe.matmul(before_ps[:, 0:SLOTS * EXPERTS], before[:], flat, start=True, stop=True)
                    pe.matmul(total_ps[:, 0:SLOTS * EXPERTS], ones[:], flat,
                              start=True, stop=True).then_inc(s_cnt, 1)
                    for s in range(SLOTS):
                        if s % SEQS == 0:
                            pe.wait_ge(r_made, s // SEQS + 1)
                            pe.wait_ge(k_made, s // SEQS + 1)
                        for n in range(2):
                            last = pe.matmul(source_ps[:, 0:TILES], hot_r[:, s, :], hot_k[:, s, n, :],
                                             start=(s == 0 and n == 0),
                                             stop=(s == SLOTS - 1 and n == 1))
                    last.then_inc(s_inv, 1)

                    def step(t, u, word):
                        r, u, v = u, u % 2, 1 - u % 2
                        if not is_int(t) or t < PAIRS:
                            pe.wait_ge(x_staged, t + 1)
                            if not is_int(t) or t >= 1:
                                pe.wait_ge(xT_ready, t)
                            pe.transpose(x_ps[:, 0:P], x_rows[u][:], ident[:]).then_inc(x_done, 1)
                        if not is_int(t) or 1 <= t <= PAIRS:
                            e = entry(pe, word, EXP_BITS, r + BACK - 1, EXPERTS - 1)
                            pe.wait_ge(xT_ready, t)
                            if not is_int(t) or t >= 3:
                                pe.wait_ge(hid_ready, t - 2)
                            pe.matmul(hid_ps[v][:], xTd[v][:],
                                      w1_sb[:, bass.ds(e, 1), :].rearrange("p o f -> p (o f)"),
                                      start=True, stop=True).then_inc(up_done, 1)
                        if not is_int(t) or 2 <= t <= PAIRS + 1:
                            pe.wait_ge(hid_ready, t - 1)
                            if not is_int(t) or t >= 4:
                                pe.wait_ge(hidT_ready, t - 3)
                            for c in range(FC):
                                last = pe.transpose(hT_ps[u][:, c * P:(c + 1) * P],
                                                    hid[u][:, c * P:(c + 1) * P], ident[:])
                            last.then_inc(hT_done2, 1)
                        if not is_int(t) or t >= 3:
                            e = entry(pe, word, EXP_BITS, r, EXPERTS - 1)
                            pe.wait_ge(hidT_ready, t - 2)
                            if not is_int(t) or t >= 5:
                                pe.wait_ge(y_read, t - 4)
                            for c in range(FC):
                                last = pe.matmul(y_ps[v][:, 0:D], hidT[v][:, c, :],
                                                 w2_sb[:, bass.ds(e, 1), c, :].rearrange(
                                                     "p o d -> p (o d)"),
                                                 start=(c == 0), stop=(c == FC - 1))
                            last.then_inc(down_done, 1)

                    pe.wait_ge(s_wx, 48)
                    pe.wait_ge(s_pairs, 1)
                    experts_word = packed_words(pe, experts_of, EXP_BITS, SPAN)
                    steps(step, pe.Fori, experts_word)

                @block.scalar
                def _(act):
                    act.wait_ge(s_inv, 1)
                    act.activation(source[:], source_ps[:, 0:TILES], ACT.Copy).then_inc(s_source, 1)

                    def stage(t, r, word, turns=0):
                        k = entry(act, word, TILE_BITS, r, TILES - 1)
                        s = (r + turns) % GROUP
                        if not is_int(t) or t < TILES:
                            act.wait_ge(gathered[s], 16 // GROUP * (t - s) + 16)
                        if not is_int(t) or t >= 2:
                            act.wait_ge(x_done, t - 1)
                        act.activation(x_rows[s % 2][:], x_sorted[:, bass.ds(k, 1), :].rearrange(
                            "p o d -> p (o d)"), ACT.Copy).then_inc(x_staged, 1)

                    def step(t, u, word):
                        r, u = u, u % 2
                        if not is_int(t) or t < PAIRS:
                            act.wait_ge(x_done, t + 1)
                            if not is_int(t) or t >= 2:
                                act.wait_ge(up_done, t - 1)
                            act.activation(xTd[u][:], x_ps[:, 0:P], ACT.Copy).then_inc(xT_ready, 1)
                        if not is_int(t) or t + 1 < PAIRS:
                            stage(t + 1, r, word, 1)
                        if not is_int(t) or 2 <= t <= PAIRS + 1:
                            act.wait_ge(hT_done2, t - 1)
                            if not is_int(t) or t >= 4:
                                act.wait_ge(down_done, t - 3)
                            act.activation(hidT[u][:].rearrange("p c t -> p (c t)"), hT_ps[u][:],
                                           ACT.Relu).then_inc(hidT_ready, 1)

                    act.wait_ge(s_pairs, 2)
                    tiles_word = packed_words(act, tiles_of, TILE_BITS, GROUP)
                    stage(0, 0, tiles_word(BACK))
                    steps(step, act.Fori, lambda t: tiles_word(t + 1 + BACK))

                @block.vector
                def _(dve):
                    order = Order(dve, s_dvec)
                    for line in (exp_line, tile_line):
                        dve.memset(line[:], 0.0)
                    order.link(dve.memset(ones_row[:], 1.0))
                    dve.wait_ge(s_cnt, 1)
                    order.link(dve.tensor_copy(total[:], total_ps[:, 0:SLOTS * EXPERTS].rearrange(
                        "p (i l e) -> p e l i", i=POS, l=SEQS)))
                    run = "p e l i -> p (e l i)"
                    order.link(dve.tensor_tensor_scan(upto[:].rearrange(run), ones_row[:],
                                                      total[:].rearrange(run), 0.0, ALU.mult, ALU.add))
                    order.link(dve.tensor_tensor(below[:].rearrange(run), upto[:].rearrange(run),
                                                 total[:].rearrange(run), ALU.subtract))
                    for e in range(EXPERTS):
                        last = dve.tensor_tensor(
                            spot[:, :, :, e],
                            before_ps[:, 0:SLOTS * EXPERTS].rearrange("p (i l e) -> p i l e", i=POS,
                                                                      l=SEQS)[:, :, :, e],
                            below[:, e].rearrange("p l i -> p i l"), ALU.add)
                    order.link(last)
                    order.link(dve.tensor_tensor(spot[:], spot[:], onehot[:], ALU.mult))
                    order.link(dve.tensor_reduce(place[:], spot[:].rearrange("p i l e -> p (i l) e"),
                                                 AX.X, ALU.add))
                    order.link(dve.tensor_scalar(place_k[:], place[:], 1.0 / P, 0.5 / P - 0.5,
                                                 ALU.mult, ALU.add))
                    order.link(dve.tensor_scalar(place_k[:], place_k[:], ROUND, None, ALU.add))
                    order.link(dve.tensor_scalar(place_k[:], place_k[:], ROUND, None, ALU.subtract))
                    order.link(dve.scalar_tensor_tensor(out=place_r[:], in0=place_k[:],
                                                        scalar=-float(P), in1=place[:],
                                                        op0=ALU.mult, op1=ALU.add))
                    for i in range(POS):
                        part = slice(i * SEQS, (i + 1) * SEQS)
                        dve.tensor_tensor(
                            is_k[:, part, :],
                            place_k[:, part].unsqueeze(2).broadcast_to([P, SEQS, TILES]),
                            p_row[:, 0:TILES].unsqueeze(1).broadcast_to([P, SEQS, TILES]),
                            ALU.is_equal).then_inc(is_k_made, 1)
                        dve.tensor_tensor(
                            hot_r[:, part, :], place_r[:, part].unsqueeze(2).broadcast_to([P, SEQS, P]),
                            p_row.unsqueeze(1).broadcast_to([P, SEQS, P]),
                            ALU.is_equal).then_inc(r_made, 1)

                    dve.tensor_copy(start, below[:, :, 0, 0])
                    order.link(dve.tensor_copy(stop, upto[:, :, SEQS - 1, POS - 1]))

                    def tiles_before(dst, bound, compare):
                        cut = cut_row.unsqueeze(1).broadcast_to([P, EXPERTS, TILES - 1])
                        order.link(dve.tensor_tensor(
                            cuts[:], bound.unsqueeze(2).broadcast_to([P, EXPERTS, TILES - 1]), cut,
                            compare))
                        order.link(dve.tensor_reduce(dst, cuts[:], AX.X, ALU.add))

                    tiles_before(jump, start, ALU.is_ge)
                    tiles_before(last_tile, stop, ALU.is_gt)
                    order.link(dve.tensor_tensor(count[:], last_tile, jump, ALU.subtract))
                    dve.tensor_tensor(last_tile, stop, start, ALU.is_gt)
                    order.link(dve.tensor_scalar(count[:], count[:], 1.0, None, ALU.add))
                    order.link(dve.tensor_tensor(count[:], count[:], last_tile, ALU.mult))
                    order.link(dve.tensor_tensor_scan(cincl[:], ones_row[:, 0:EXPERTS], count[:], 0.0,
                                                      ALU.mult, ALU.add))
                    order.link(dve.tensor_tensor(count[:], cincl[:], count[:], ALU.subtract))
                    order.link(dve.tensor_tensor(jump, jump, count[:], ALU.subtract))

                    def by_pair(v):
                        return v.unsqueeze(2).broadcast_to([P, PAIRS, EXPERTS])

                    def by_expert(v):
                        return v.unsqueeze(1).broadcast_to([P, PAIRS, EXPERTS])

                    def pack(dst, line, bits, n, done):
                        width = WORDS
                        word = line[:, n - 1:n - 1 + width]
                        for k in range(n - 2, -1, -1):
                            into = packed[k % 2][:]
                            order.link(dve.scalar_tensor_tensor(
                                out=into, in0=word, scalar=float(1 << bits),
                                in1=line[:, k:k + width], op0=ALU.mult, op1=ALU.add))
                            word = into
                        dve.tensor_copy(dst[:], word).then_inc(done, 1)

                    order.link(dve.tensor_tensor(tmp[:], by_pair(q_row), by_expert(cincl[:]), ALU.is_ge))
                    order.link(dve.tensor_reduce(expf, tmp[:], AX.X, ALU.add))
                    order.link(dve.tensor_scalar(expf, expf, EXPERTS - 1.0, None, ALU.min))
                    order.link(dve.tensor_tensor(sel[:], by_pair(expf), by_expert(e_row),
                                                 ALU.is_equal))
                    pack(experts_of, exp_line, EXP_BITS, SPAN, s_pairs)
                    def of_expert(dst, src):
                        order.link(dve.tensor_tensor(tmp[:], sel[:], by_expert(src), ALU.mult))
                        order.link(dve.tensor_reduce(dst, tmp[:], AX.X, ALU.add))

                    of_expert(tilef, jump)
                    order.link(dve.tensor_tensor(tilef, tilef, q_row, ALU.add))
                    order.link(dve.tensor_scalar(tilef, tilef, TILES - 1.0, None, ALU.min))
                    pack(tiles_of, tile_line, TILE_BITS, GROUP, s_pairs)
                    of_expert(first_row[:], start)
                    of_expert(stop_row[:], stop)
                    order.link(dve.tensor_scalar(row[:], tilef, float(P), p_col, ALU.mult, ALU.add))
                    dve.tensor_tensor(first_row[:], row[:], first_row[:], ALU.is_ge)
                    order.link(dve.tensor_tensor(stop_row[:], row[:], stop_row[:], ALU.is_lt))
                    order.link(dve.tensor_tensor(first_row[:], first_row[:], stop_row[:], ALU.mult))
                    order.link(dve.tensor_scalar(row[:], q_row, cincl[:, EXPERTS - 1:], None, ALU.is_lt))
                    order.link(dve.tensor_tensor(owned[:], first_row[:], row[:], ALU.mult))

                    def step(t, u, word):
                        r, u, v = u, u % 2, 1 - u % 2
                        experts, tiles = word
                        if not is_int(t) or 1 <= t <= PAIRS:
                            e = entry(dve, experts, EXP_BITS, r + BACK - 1, EXPERTS - 1)
                            dve.wait_ge(up_done, t)
                            if not is_int(t) or t >= 3:
                                dve.wait_ge(hT_done2, t - 2)
                            dve.tensor_tensor(hid[v][:], hid_ps[v][:],
                                              b1_sb[:, bass.ds(e, 1), :].rearrange("p o f -> p (o f)"),
                                              ALU.add).then_inc(hid_ready, 1)
                        if not is_int(t) or t >= 3:
                            e = entry(dve, experts, EXP_BITS, r, EXPERTS - 1)
                            k = entry(dve, tiles, TILE_BITS, r, TILES - 1)
                            dve.wait_ge(down_done, t - 2)
                            if not is_int(t) or t >= 4:
                                dve.wait_ge(y_added, t - 3)
                            dve.tensor_tensor(yb[:], y_ps[v][:, 0:D],
                                              b2_sb[:, bass.ds(e, 1), :].rearrange("p o d -> p (o d)"),
                                              ALU.add).then_inc(y_read, 1)
                            dve.wait_ge(y_read, t - 2)
                            y_tile = y[:, bass.ds(k, 1), :].rearrange("p o d -> p (o d)")
                            dve.scalar_tensor_tensor(out=y_tile, in0=yb[:],
                                                     scalar=owned[:, bass.ds(t - 3, 1)], in1=y_tile,
                                                     op0=ALU.mult, op1=ALU.add).then_inc(y_added, 1)

                    dve.wait_ge(s_wx, 48)
                    dve.wait_ge(b1_loaded, 16)
                    dve.wait_ge(y_loaded, 32)
                    dve.wait_ge(s_pairs, 2)
                    experts_word = packed_words(dve, experts_of, EXP_BITS, SPAN)
                    tiles_word = packed_words(dve, tiles_of, TILE_BITS, GROUP)
                    steps(step, dve.Fori, lambda t: (experts_word(t), tiles_word(t)))


def kernel(x, L0_tok_kernel, L0_ffn_Wa, L0_ffn_ba, L0_ffn_Ws, L0_ffn_bs, L1_attn_W, L1_attn_b,
           L1_ffn_Wg, L1_ffn_bg, L1_ffn_W1, L1_ffn_b1, L1_ffn_W2, L1_ffn_b2):
    import numpy as _np
    import concourse.bacc as _bacc
    from concourse import mybir as _mybir
    from concourse.bass_utils import run_bass_kernel_spmd as _run

    nc = _bacc.Bacc("TRN2", target_bir_lowering=False, num_devices=1)
    laid_out = {
        "xT": _np.asarray(x).transpose(0, 2, 1),
        "tok_w": _np.asarray(L0_tok_kernel).transpose(1, 0, 2),
        "qkv_w": _np.asarray(L1_attn_W).T,
        "qkv_b": _np.asarray(L1_attn_b),
        "gate_w": _np.asarray(L1_ffn_Wg),
        "gate_b": _np.asarray(L1_ffn_bg),
        "w1": _np.asarray(L1_ffn_W1).transpose(1, 0, 2),
        "b1": _np.asarray(L1_ffn_b1),
        "w2": _np.asarray(L1_ffn_W2).reshape(EXPERTS, FC, P, D).transpose(2, 0, 1, 3),
        "b2": _np.asarray(L1_ffn_b2),
    }
    arrays, args = {}, []
    for name, a in laid_out.items():
        a = _np.ascontiguousarray(a)
        arrays[name] = a
        args.append(nc.dram_tensor(name, a.shape, _mybir.dt.from_np(a.dtype), kind="ExternalInput").ap())
    args.append(nc.dram_tensor("out", (TOKENS, D), _mybir.dt.float32, kind="ExternalOutput").ap())
    build(nc, *args)
    r = _run(nc, [arrays], core_ids=[0])
    return r.results[0]["out"].reshape(SEQS, T, D)
```
